# Optimizing a Trainium2 kernel written in Bass

```python
import numpy as np
import jax
import jax.numpy as jnp

def _softmax(x, axis=-1):
    return jax.nn.softmax(x, axis=axis)

def _gelu(x):
    return jax.nn.gelu(x, approximate=True)

def _silu(x):
    return jax.nn.silu(x)

def _sigmoid(x):
    return jax.nn.sigmoid(x)

def _layernorm(x, axis=-1, eps=1e-05):
    m = jnp.mean(x, axis=axis, keepdims=True)
    v = jnp.var(x, axis=axis, keepdims=True)
    return (x - m) / jnp.sqrt(v + eps)

def _scatter_add(tgt, idx, src, axis=0):
    return tgt.at[idx].add(src)

def _segment_sum(src, seg, n):
    return jax.ops.segment_sum(src, seg, n)
kernel_name = 'mk_prb_d1_jaxref_r4_cf94fd'

def setup_inputs(seed: int=0):
    np.random.seed(seed)
    _w = jnp.asarray

    def _L0_attn_setup():
        import jax, jax.numpy as jnp
        import numpy as np
        N_HEAD = 16
        CHUNK = 128

        def _phi(x):
            return jax.nn.elu(x) + 1.0

        def _causal_linear_attn(qp, kp, v):
            B, H, T, D = qp.shape
            NC = T // CHUNK

            def to_chunks(a):
                return a.reshape(B, H, NC, CHUNK, D).transpose(2, 0, 1, 3, 4)
            qc, kc, vc = (to_chunks(qp), to_chunks(kp), to_chunks(v))
            mask = jnp.tril(jnp.ones((CHUNK, CHUNK), dtype=bool))

            def step(carry, blk):
                S, z = carry
                q_c, k_c, v_c = blk
                scores = jnp.einsum('bhcd,bhkd->bhck', q_c, k_c)
                scores = jnp.where(mask, scores, 0.0)
                num = jnp.einsum('bhck,bhke->bhce', scores, v_c) + jnp.einsum('bhcd,bhde->bhce', q_c, S)
                den = scores.sum(-1) + jnp.einsum('bhcd,bhd->bhc', q_c, z)
                S = S + jnp.einsum('bhkd,bhke->bhde', k_c, v_c)
                z = z + k_c.sum(axis=2)
                return ((S, z), (num, den))
            S0 = jnp.zeros((B, H, D, D), dtype=qp.dtype)
            z0 = jnp.zeros((B, H, D), dtype=qp.dtype)
            _, (num, den) = jax.lax.scan(step, (S0, z0), (qc, kc, vc))
            y = num / (den[..., None] + 1e-06)
            y = y.transpose(1, 2, 0, 3, 4).reshape(B, H, T, D)
            return y
        key = jax.random.key(seed)
        k1, k2, k3 = jax.random.split(key, 3)
        B, T, E = (4, 512, 256)
        x = jax.random.normal(k1, (B, T, E), dtype=jnp.float32)
        w_attn = jax.random.normal(k2, (3 * E, E), dtype=jnp.float32) * 0.02
        w_proj = jax.random.normal(k3, (E, E), dtype=jnp.float32) * 0.02
        return {'x': x, 'w_attn': w_attn, 'w_proj': w_proj}
    _L0_attn_in = _L0_attn_setup()

    def _L0_ffn_setup():
        import jax, jax.numpy as jnp
        import numpy as np
        D_MODEL = 256
        D_FF = 1024
        NUM_EXPERTS = 8
        key = jax.random.key(seed)
        ks = jax.random.split(key, 8)
        scale_in = 1.0 / np.sqrt(D_MODEL)
        scale_ff = 1.0 / np.sqrt(D_FF)
        x = jax.random.normal(ks[0], (4, 512, D_MODEL), dtype=jnp.float32)
        gate_w = jax.random.uniform(ks[1], (NUM_EXPERTS, D_MODEL), jnp.float32, -scale_in, scale_in)
        gate_b = jax.random.uniform(ks[2], (NUM_EXPERTS,), jnp.float32, -scale_in, scale_in)
        expert_bias = jnp.zeros((NUM_EXPERTS,), dtype=jnp.float32)
        w1 = jax.random.uniform(ks[3], (NUM_EXPERTS, D_MODEL, D_FF), jnp.float32, -scale_in, scale_in)
        b1 = jax.random.uniform(ks[4], (NUM_EXPERTS, D_FF), jnp.float32, -scale_in, scale_in)
        w2 = jax.random.uniform(ks[5], (NUM_EXPERTS, D_FF, D_MODEL), jnp.float32, -scale_ff, scale_ff)
        b2 = jax.random.uniform(ks[6], (NUM_EXPERTS, D_MODEL), jnp.float32, -scale_ff, scale_ff)
        return {'x': x, 'gate_w': gate_w, 'gate_b': gate_b, 'expert_bias': expert_bias, 'w1': w1, 'b1': b1, 'w2': w2, 'b2': b2}
    _L0_ffn_in = _L0_ffn_setup()
    _d = {'L0_attn_x': _L0_attn_in['x'], 'L0_attn_w_attn': _L0_attn_in['w_attn'], 'L0_attn_w_proj': _L0_attn_in['w_proj'], 'L0_ffn_gate_w': _L0_ffn_in['gate_w'], 'L0_ffn_gate_b': _L0_ffn_in['gate_b'], 'L0_ffn_expert_bias': _L0_ffn_in['expert_bias'], 'L0_ffn_w1': _L0_ffn_in['w1'], 'L0_ffn_b1': _L0_ffn_in['b1'], 'L0_ffn_w2': _L0_ffn_in['w2'], 'L0_ffn_b2': _L0_ffn_in['b2']}
    _x0 = _d['L0_attn_x']
    _d['L0_attn_x'] = jax.random.normal(jax.random.fold_in(jax.random.key(seed), 1), (4, 1024, 256), dtype=_x0.dtype)
    del _x0
    return _d

def reference(L0_attn_x, L0_attn_w_attn, L0_attn_w_proj, L0_ffn_gate_w, L0_ffn_gate_b, L0_ffn_expert_bias, L0_ffn_w1, L0_ffn_b1, L0_ffn_w2, L0_ffn_b2):

    def _L0_attn_ref(x, w_attn, w_proj):
        import jax, jax.numpy as jnp
        import numpy as np
        N_HEAD = 16
        CHUNK = 128

        def _phi(x):
            return jax.nn.elu(x) + 1.0

        def _causal_linear_attn(qp, kp, v):
            B, H, T, D = qp.shape
            NC = T // CHUNK

            def to_chunks(a):
                return a.reshape(B, H, NC, CHUNK, D).transpose(2, 0, 1, 3, 4)
            qc, kc, vc = (to_chunks(qp), to_chunks(kp), to_chunks(v))
            mask = jnp.tril(jnp.ones((CHUNK, CHUNK), dtype=bool))

            def step(carry, blk):
                S, z = carry
                q_c, k_c, v_c = blk
                scores = jnp.einsum('bhcd,bhkd->bhck', q_c, k_c)
                scores = jnp.where(mask, scores, 0.0)
                num = jnp.einsum('bhck,bhke->bhce', scores, v_c) + jnp.einsum('bhcd,bhde->bhce', q_c, S)
                den = scores.sum(-1) + jnp.einsum('bhcd,bhd->bhc', q_c, z)
                S = S + jnp.einsum('bhkd,bhke->bhde', k_c, v_c)
                z = z + k_c.sum(axis=2)
                return ((S, z), (num, den))
            S0 = jnp.zeros((B, H, D, D), dtype=qp.dtype)
            z0 = jnp.zeros((B, H, D), dtype=qp.dtype)
            _, (num, den) = jax.lax.scan(step, (S0, z0), (qc, kc, vc))
            y = num / (den[..., None] + 1e-06)
            y = y.transpose(1, 2, 0, 3, 4).reshape(B, H, T, D)
            return y
        B, T, E = x.shape
        H = N_HEAD
        D = E // H
        qkv = x @ w_attn.T
        q, k, v = jnp.split(qkv, 3, axis=2)

        def heads(a):
            return a.reshape(B, T, H, D).transpose(0, 2, 1, 3)
        y = _causal_linear_attn(_phi(heads(q)), _phi(heads(k)), heads(v))
        y = y.transpose(0, 2, 1, 3).reshape(B, T, E)
        return y @ w_proj.T

    def _L0_ffn_ref(x, gate_w, gate_b, expert_bias, w1, b1, w2, b2):
        import jax, jax.numpy as jnp
        import numpy as np
        D_MODEL = 256
        D_FF = 1024
        NUM_EXPERTS = 8
        gate_logits = jnp.einsum('bsd,ed->bse', x, gate_w) + gate_b + expert_bias
        top_idx = jnp.argmax(gate_logits, axis=-1)
        out = jnp.zeros_like(x)
        for e in range(NUM_EXPERTS):
            mask = (top_idx == e)[..., None].astype(x.dtype)
            h = jax.nn.relu(jnp.einsum('bsd,df->bsf', x, w1[e]) + b1[e])
            y = jnp.einsum('bsf,fd->bsd', h, w2[e]) + b2[e]
            out = out + mask * y
        return out
    x = L0_attn_x
    xn = _layernorm(x, axis=-1)
    x = x + _L0_attn_ref(xn, L0_attn_w_attn, L0_attn_w_proj) + _L0_ffn_ref(xn, L0_ffn_gate_w, L0_ffn_gate_b, L0_ffn_expert_bias, L0_ffn_w1, L0_ffn_b1, L0_ffn_w2, L0_ffn_b2)
    return x

_drawn_inputs = setup_inputs


def setup_inputs(seed=0):
    import zlib

    import numpy as np

    out = dict(_drawn_inputs(seed))
    spreads = {'L0_ffn_expert_bias': (0.0, 0.1)}
    factors = {'L0_attn_w_attn': 6.716, 'L0_attn_w_proj': 6.563, 'L0_ffn_b1': 3.975, 'L0_ffn_b2': 3.165}
    for name, (base, spread) in spreads.items():
        noise = np.random.default_rng([zlib.crc32(name.encode()), seed]).standard_normal(out[name].shape)
        drawn = base * np.exp(spread * noise) if base else spread * noise
        out[name] = jnp.asarray(drawn.astype(out[name].dtype))
    for name, factor in factors.items():
        out[name] = (out[name] * factor).astype(out[name].dtype)
    return out
```

```python
from contextlib import ExitStack

import concourse.bass as bass
from concourse import mybir

F32 = mybir.dt.float32
F16 = mybir.dt.float16
BF16 = mybir.dt.bfloat16
I32 = mybir.dt.int32
ALU = mybir.AluOpType
ACT = mybir.ActivationFunctionType
X_AX = mybir.AxisListType.X

B, T, D = 4, 1024, 256
NT = B * T
NC = NT // 128
CPB = T // 128
H = 16
E = 8
F = 1024
NS = NT // 128 + E - 1
XSH = 10

C_ID, C_MASK, C_BD, C_HM, C_WT, C_SL, C_T, C_N = (0, 128, 256, 384, 392, 400, 439, 440)
D_RST, D_P, D_C32, D_N = (0, 256, 384, 416)


class Engine:

    def __init__(self, sem):
        self.sem, self.count, self.items, self.seen = sem, 0, [], {}

    def wait(self, *tokens):
        for t in tokens:
            if t is None:
                continue
            sem, v = t
            if self.seen.get(id(sem), 0) < v:
                self.seen[id(sem)] = v
                self.items.append(lambda e, sem=sem, v=v: e.wait_ge(sem, v))

    def do(self, fn, *tokens, sig=True):
        self.wait(*tokens)
        if sig:
            self.count += 1
            self.items.append(lambda e: fn(e).then_inc(self.sem, 1))
            return (self.sem, self.count)
        self.items.append(fn)
        return None

    def dma(self, fn, slot, *tokens):
        self.wait(*tokens)
        slot.count += 16
        self.items.append(lambda e: fn(e).then_inc(slot.sem, 16))
        return (slot.sem, slot.count)

    def run(self, e):
        for f in self.items:
            f(e)


class Slot:

    def __init__(self, sem):
        self.sem, self.count = sem, 0


def program(nc, x, wall, wp, gb, eb, w1, b1, w2, b2, cst, cst2, tri, out):
    ctx = ExitStack()
    with ctx:
        def sb(name, shape, dt):
            return ctx.enter_context(nc.sbuf_tensor(name, shape, dt))

        def sem(name):
            return ctx.enter_context(nc.semaphore(name))

        def slot(name):
            return Slot(sem(name))

        PS = [ctx.enter_context(nc.psum_tensor(f"ps{i}", [128, 512], F32)) for i in range(8)]

        W = sb("W", [128, E * 8192], F16)
        ST = sb("ST", [128, 4096], F32)
        CT = sb("CT", [128, C_N], F32)
        XR = [sb(f"XR{i}", [128, 512], F32) for i in range(3)]
        xT = sb("xT", [128, 2, 128], F32)
        WA = sb("WA", [128, 2, 776], F32)
        WP = sb("WP", [128, 2, 256], F32)
        QK = sb("QK", [128, 512], F32)
        VB = [sb(f"VB{i}", [128, 16 * 128], F32) for i in range(2)]
        qkT = sb("qkT", [128, 4, 128], F32)
        QM = sb("QM", [128, 16, 128], F32)
        SM = sb("SM", [128, 16, 128], F32)
        CU = sb("CU", [128, 2, 128], F32)
        PR = sb("PR", [128, 2, 128], F32)
        RC = sb("RC", [128, 256], F32)
        yT = sb("yT", [128, 2, 128], F32)
        SS = sb("SS", [128, 2, 128], F32)
        L = sb("L", [128, NC, E], F32)
        GBE = sb("GBE", [128, 2, E], F32)
        st6 = sb("st6", [128, 6], F32)
        mv = sb("mv", [128, 2], F32)
        rs = sb("rs", [128, 1], F32)
        nv = sb("nv", [128, 4], F32)
        nvi = sb("nvi", [128, 1], I32)
        tri16 = sb("tri16", [128, 128], BF16)
        one16 = sb("one16", [128, 128], BF16)
        id16 = sb("id16", [128, 128], F16)
        B1 = sb("B1", [128, E, 8], F32)
        B1S = sb("B1S", [128, E * 8], F32)
        MX = sb("MX", [128, E, 2], F32)
        MXA = sb("MXA", [128, E, 2], F32)
        BM = sb("BM", [128, E], F32)
        BMA = sb("BMA", [128, E], F32)
        ea = sb("ea", [128, E, 2], I32)
        eb1 = sb("eb1", [128, E], I32)
        Eh = sb("Eh", [128, E], I32)
        ti = sb("ti", [128, E, 4], I32)
        SC = sb("SC", [128, E, 4], I32)
        TA = sb("TA", [128, E], F32)
        TG = sb("TG", [128, E], F32)
        es = sb("es", [128, NS], I32)
        ids = sb("ids", [128, NS], I32)

        scr = nc.dram_tensor("scr", [NT, 512], F32, kind="Internal").ap()
        outr = out.rearrange("b t d -> (b t) d")
        xr = x.rearrange("b t d -> (b t) d")

        pe, ve, ac, po, sp = (Engine(sem(n)) for n in ("s_pe", "s_ve", "s_ac", "s_po", "s_sp"))

        def cc(a, n, p=128):
            return CT[0:p, a:a + n]

        k_ct, k_wa, k_wp, k_sm = slot("k_ct"), slot("k_wa"), slot("k_wp"), slot("k_sm")
        k_x = [slot(f"k_x{i}") for i in range(3)]
        k_st = slot("k_st")
        k_scr = [slot(f"k_scr{i}") for i in range(3)]

        def load_x(c):
            return sp.dma(lambda e: e.dma_start(XR[c % 3][:, 256:512], xr[c * 128:(c + 1) * 128, :]),
                          k_x[c % 3], *t_free.get(c, ()))

        t_free = {}
        t_x = {}
        t_x[0] = load_x(0)
        t_ct = sp.dma(lambda e: e.dma_start(CT[:, :], cst), k_ct)
        t_wa = sp.dma(lambda e: e.dma_start(WA[:, :, :], wall), k_wa)
        t_x[1] = load_x(1)
        t_gb = sp.dma(lambda e: e.dma_start(GBE[:, 0, :], gb), k_sm)
        t_eb = sp.dma(lambda e: e.dma_start(GBE[:, 1, :], eb), k_sm)
        t_b1 = sp.dma(lambda e: e.dma_start(B1[:, :, :], b1), k_sm)
        t_wp = sp.dma(lambda e: e.dma_start(WP[:, :, :], wp), k_wp)

        z0 = po.do(lambda e: e.memset(VB[0][:, :], 0.0))
        z1 = po.do(lambda e: e.memset(VB[1][:, :], 0.0))
        t_zv = [z0, z1]
        t_one = po.do(lambda e: e.memset(one16[:, :], 1.0))
        t_tr = sp.dma(lambda e: e.dma_start(QM[:, 0, :], tri), slot("k_tri"))
        t_tri = po.do(lambda e: e.tensor_copy(tri16[:, :], QM[:, 0, :]), t_tr)
        t_id16 = po.do(lambda e: e.tensor_copy(id16[:, :], cc(C_ID, 128)), t_ct)

        def load_w(ex, *tokens):
            a = sp.dma(lambda e: e.dma_start(ST[:, 0:2048], w1[ex]), k_st, *tokens)
            b = sp.dma(lambda e: e.dma_start(ST[:, 2048:4096], w2[ex]), k_st)
            return b

        t_st = load_w(0)

        tk = {}

        def g(what, c):
            return tk.get((what, c))

        def stage_norm(c):
            xb = XR[c % 3]
            a = ve.do(lambda e: e.bn_stats(st6[:, :], xb[:, 256:512]), t_x[c])
            a = ve.do(lambda e: e.bn_aggr(mv[:, :], st6[:, :]), a)
            a = ve.do(lambda e: e.tensor_scalar(nv[:, 0:1], mv[:, 1:2], 1e-5, None, ALU.add), a)
            a = ve.do(lambda e: e.tensor_scalar(nvi[:, 0:1], nv[:, 0:1].bitcast(I32), 1, None,
                                                ALU.logical_shift_right), a)
            a = ve.do(lambda e: e.tensor_scalar(rs[:, :].bitcast(I32), nvi[:, 0:1], -1.0, float(0x5f3759df),
                                                ALU.mult, ALU.add), a)
            for _ in range(3):
                a = po.do(lambda e: e.tensor_scalar(nv[:, 1:2], rs[:, :], rs[:, 0:1], nv[:, 0:1],
                                                    ALU.mult, ALU.mult), a)
                a = po.do(lambda e: e.tensor_scalar(nv[:, 2:3], nv[:, 1:2], -0.5, 1.5, ALU.mult, ALU.add), a)
                a = po.do(lambda e: e.tensor_tensor(rs[:, :], rs[:, :], nv[:, 2:3], ALU.mult), a)
            tk["rs", c] = a

        def stage_xn(c):
            xb = XR[c % 3]
            tk["xn", c] = ve.do(lambda e: e.tensor_scalar(
                xb[:, 0:256], xb[:, 256:512], mv[:, 0:1], rs[:, 0:1], ALU.subtract, ALU.mult),
                tk["rs", c])

        def pe_xt(c):
            for k in range(2):
                a = pe.do(lambda e, k=k: e.transpose(PS[7][:, k * 128:(k + 1) * 128],
                                                     XR[c % 3][:, k * 128:(k + 1) * 128], cc(C_ID, 128)),
                          g("xn", c), t_ct, g("res", c - 2), g("xT", c - 1), sig=(k == 1))
            tk["pxT", c] = a
            tk["xT", c] = ac.do(lambda e: e.activation(
                xT[:, :, :], PS[7][:, 0:256].rearrange("p (k n) -> p k n", k=2), ACT.Copy),
                a, g("pvg", c - 1))

        def pe_qk(c):
            for k in range(2):
                a = pe.do(lambda e, k=k: e.matmul(PS[0][:, :], xT[:, k, :], WA[:, k, 0:512],
                                                  start=(k == 0), stop=(k == 1)),
                          t_wa, g("xT", c), g("qk", c - 1), sig=(k == 1))
            tk["pqk", c] = a
            tk["re", c] = ac.do(lambda e: e.activation(QK[:, :], PS[0][:, :], ACT.Relu), a,
                                g("pqT", c - 1), g("pst", c - 1))
            tk["ex", c] = ac.do(lambda e: e.activation(PS[0][:, :], PS[0][:, :], ACT.Exp), tk["re", c])
            tk["qk", c] = ve.do(lambda e: e.scalar_tensor_tensor(
                QK[:, :], PS[0][:, :], 1.0, QK[:, :], ALU.min, ALU.add), tk["ex", c])

        def pe_vg(c):
            for k in range(2):
                a = pe.do(lambda e, k=k: e.matmul(PS[1][:, 0:264], xT[:, k, :], WA[:, k, 512:776],
                                                  start=(k == 0), stop=(k == 1)),
                          g("xT", c), g("lg", c - 1), sig=(k == 1))
            tk["pvg", c] = a
            vb = VB[c % 2]
            for q in range(2):
                dst = vb[:, q * 1024:(q + 1) * 1024]
                dst = bass_diag(dst)
                b = ve.do(lambda e, q=q, dst=dst: e.tensor_copy(
                    dst, PS[1][:, q * 128:(q + 1) * 128].rearrange("p (h e) -> p h e", h=8)),
                    a, t_zv[c % 2], g("ppv", c - 2), g("pst", c - 2))
            tk["v", c] = b
            tk["lg", c] = ve.do(lambda e: e.tensor_tensor(L[:, c, :], PS[1][:, 256:264], GBE[:, 0, :], ALU.add),
                                t_gb, t_b1)

        def bass_diag(ap):
            return ap.rearrange("p (h e) -> p h e", h=8)[:, :, 0:16]

        def pe_tr(c):
            for i in range(4):
                a = pe.do(lambda e, i=i: e.transpose(PS[2][:, i * 128:(i + 1) * 128],
                                                     QK[:, i * 128:(i + 1) * 128], cc(C_ID, 128)),
                          g("qk", c), g("qm0", c - 1), g("qkT", c - 1), sig=(i == 3))
            tk["pqT", c] = a
            tk["qkT", c] = ac.do(lambda e: e.activation(
                qkT[:, :, :], PS[2][:, :].rearrange("p (k n) -> p k n", k=4), ACT.Copy),
                a, g("ppv", c - 1), g("cum", c - 1), g("pr", c - 1))
            qa = qkT[:, 0:1, :].broadcast_to((128, 8, 128))
            hm = cc(C_HM, 8).rearrange("p (h o) -> p h o", o=1).broadcast_to((128, 8, 128))
            tk["qm0", c] = ve.do(lambda e: e.tensor_tensor(QM[:, 0:8, :], qa, hm, ALU.mult),
                                 tk["qkT", c], g("psc", c - 1), t_tri)
            for h in range(8):
                b = ac.do(lambda e, h=h: e.activation(QM[:, 8 + h, :], qkT[:, 1, :], ACT.Copy,
                                                      scale=cc(C_HM + h, 1)), tk["qkT", c], g("psc", c - 1),
                          sig=(h == 7))
            tk["qm1", c] = b
            for q in range(2):
                init = 0.0 if c % CPB == 0 else CL[:, q:q + 1]
                tk["cum", c] = ve.do(lambda e, q=q, init=init: e.tensor_tensor_scan(
                    CU[:, q, :], onef[:, :], qkT[:, 2 + q, :], init, ALU.mult, ALU.add),
                    t_onef, g("cl", c - 1), g("pr", c - 1))
            tk["cl", c] = ve.do(lambda e: e.tensor_copy(CL[:, :], CU[:, :, 127]), tk["cum", c])
            tk["pr", c] = po.do(lambda e: e.tensor_tensor(PR[:, :, :], CU[:, :, :], qkT[:, 0:2, :], ALU.mult),
                                tk["cum", c], tk["qkT", c], g("pden", c - 1))

        def pe_sc(c, i):
            bank = PS[3 + i % 2]
            gr = i // 2
            a = pe.do(lambda e: e.matmul(bank[:, :], qkT[:, 2 + gr, :],
                                         QM[:, 4 * i:4 * i + 4, :].rearrange("p h n -> p (h n)"),
                                         start=True, stop=True),
                      g("qkT", c), g("qm0", c) if gr == 0 else g("qm1", c), t_tri,
                      g("sm", (c, i - 2)) if i >= 2 else g("sm", (c - 1, i + 2)))
            if i == 3:
                tk["psc", c] = a
            msk = CT[:, C_MASK:C_MASK + 128].rearrange("p (o n) -> p o n", o=1).broadcast_to((128, 4, 128))
            tk["sm", (c, i)] = ve.do(lambda e: e.tensor_tensor(
                SM[:, 4 * i:4 * i + 4, :], bank[:, :].rearrange("p (h n) -> p h n", h=4), msk, ALU.mult),
                a, g("ppv", c - 1))

        def pe_pv(c, q):
            first = c % CPB == 0
            vb = VB[c % 2]
            dst = PS[5][:, q * 128:(q + 1) * 128]
            if not first:
                pe.do(lambda e: e.matmul(dst, SS[:, q, :], qkT[:, q, :], start=True, stop=False),
                      g("ss", c - 1), g("y", c - 1), sig=False)
            for h in range(8):
                hh = 8 * q + h
                a = pe.do(lambda e, h=h, hh=hh: e.matmul(
                    dst, vb[:, q * 1024 + h * 112:q * 1024 + h * 112 + 128], SM[:, hh, :],
                    start=(first and h == 0), stop=(h == 7)),
                    g("v", c), g("sm", (c, hh // 4)), g("y", c - 1), sig=(h == 7))
            if q == 1:
                tk["ppv", c] = a

        def pe_den(c):
            a = pe.do(lambda e: e.matmul(PS[5][:, 256:512], cc(C_BD, 128),
                                         PR[:, :, :].rearrange("p q n -> p (q n)"), start=True, stop=True),
                      g("pr", c), g("y", c - 1))
            tk["pden", c] = a
            b = ve.do(lambda e: e.tensor_scalar(RC[:, :], PS[5][:, 256:512], 1e-6, None, ALU.add),
                      a, g("ppv", c))
            b = ve.do(lambda e: e.reciprocal(RC[:, :], RC[:, :]), b)
            tk["y", c] = ve.do(lambda e: e.tensor_tensor(
                yT[:, :, :], PS[5][:, 0:256].rearrange("p (q n) -> p q n", q=2),
                RC[:, :].rearrange("p (q n) -> p q n", q=2), ALU.mult), b, g("ppr", c - 1))

        def pe_state(c):
            if c % CPB == CPB - 1:
                return
            for q in range(2):
                vd = bass_diag(VB[c % 2][:, q * 1024:(q + 1) * 1024])
                a = pe.do(lambda e, q=q, vd=vd: e.matmul(
                    PS[6][:, q * 128:(q + 1) * 128], QK[:, 256 + q * 128:384 + q * 128], vd,
                    start=(c % CPB == 0 and q == 0), stop=True, skip_group_check=True),
                    g("v", c), g("qk", c), g("ss", c - 1), g("ss", c - 2), sig=(q == 1))
            tk["pst", c] = a

        def ss_copy(c):
            if c % CPB == CPB - 1:
                return
            a = g("pst", c)
            tk["ss", c] = ve.do(lambda e: e.tensor_tensor(
                SS[:, :, :], PS[6][:, 0:256].rearrange("p (q n) -> p q n", q=2),
                cc(C_BD, 128).rearrange("p (q n) -> p q n", q=1).broadcast_to((128, 2, 128)), ALU.mult), a, g("ppv", c))

        def pe_proj(c):
            for q in range(2):
                a = pe.do(lambda e, q=q: e.matmul(PS[7][:, 256:512], yT[:, q, :], WP[:, q, :],
                                                  start=(q == 0), stop=(q == 1)),
                          t_wp, g("y", c), g("xT", c + 1), sig=(q == 1))
            tk["ppr", c] = a
            xb = XR[c % 3]
            tk["res", c] = ve.do(lambda e: e.tensor_tensor(xb[:, 256:512], xb[:, 256:512],
                                                           PS[7][:, 256:512], ALU.add), a)
            tk["st", c] = sp.dma(lambda e: e.dma_start(scr[c * 128:(c + 1) * 128, :], xb[:, :]),
                                 k_scr[c % 3], tk["res", c])
            t_free[c + 3] = (tk["st", c], g("pxT", c))
            if c + 3 < NC:
                t_x[c + 3] = load_x(c + 3)

        tw = {}

        def weights(c):
            nonlocal t_st
            ex, ph = c // 4, c % 4
            o = ex * 8192
            if ph == 0:
                for i in range(2):
                    a = ve.do(lambda e, i=i: e.tensor_reduce(MX[:, ex, i:i + 1], ST[:, i * 2048:(i + 1) * 2048],
                                                             X_AX, ALU.max, apply_absolute_value=True), t_st)
                tw["max"] = po.do(lambda e: e.partition_all_reduce(
                    MXA[:, ex, :], MX[:, ex, :], 128, bass.bass_isa.ReduceOp.max), a)
            if ph == 1:
                a = ve.do(lambda e: e.tensor_scalar(ea[:, ex, :], MXA[:, ex, :].bitcast(I32), 23, None,
                                                    ALU.logical_shift_right), tw["max"])
                a = ve.do(lambda e: e.tensor_scalar(ea[:, ex, :], ea[:, ex, :], 80, 240, ALU.max, ALU.min), a)
                b = ve.do(lambda e: e.scalar_tensor_tensor(
                    Eh[:, ex:ex + 1], ea[:, ex, 0:1], 9.0, eb1[:, ex:ex + 1], ALU.add, ALU.max), a, t_eb1)
                ve.do(lambda e: e.tensor_scalar(ti[:, ex, 0:2], ea[:, ex, :], -1.0, 268.0, ALU.mult, ALU.add))
                ve.do(lambda e: e.tensor_scalar(ti[:, ex, 2:3], Eh[:, ex:ex + 1], -1.0, 268.0,
                                                ALU.mult, ALU.add), b)
                a = ve.do(lambda e: e.scalar_tensor_tensor(
                    TAi[:, ex, 0:1], ea[:, ex, 0:1], 117.0, Eh[:, ex:ex + 1], ALU.add, ALU.subtract))
                a = ve.do(lambda e: e.scalar_tensor_tensor(
                    TAi[:, ex, 1:2], ea[:, ex, 1:2], -155.0, Eh[:, ex:ex + 1], ALU.add, ALU.add))
                a = ve.do(lambda e: e.tensor_scalar(TAi[:, ex, :], TAi[:, ex, :], 1, 254, ALU.max, ALU.min), a)
                ve.do(lambda e: e.tensor_scalar(SC[:, ex, 0:3], ti[:, ex, 0:3], 23, None,
                                                ALU.logical_shift_left), a)
                a = ve.do(lambda e: e.tensor_scalar(TAs[:, ex, :], TAi[:, ex, :], 23, None,
                                                    ALU.logical_shift_left), a)
                tw["sc"] = ve.do(lambda e: e.tensor_scalar(
                    B1S[:, ex * 8:(ex + 1) * 8], B1[:, ex, :], SC[:, ex, 2:3].bitcast(F32), None, ALU.mult), a)
            if ph in (1, 2):
                i = ph - 1
                src = ST[:, i * 2048:(i + 1) * 2048]
                s = SC[:, ex, i:i + 1].bitcast(F32)
                hi = W[:, o + i * 4096:o + i * 4096 + 2048]
                lo = W[:, o + i * 4096 + 2048:o + i * 4096 + 4096]
                a = ac.do(lambda e: e.activation(hi, src, ACT.Copy, scale=s), tw["sc"])
                a = ve.do(lambda e: e.scalar_tensor_tensor(lo, src, s, hi, ALU.mult, ALU.subtract), a)
                tw["w", ex] = a
            if ph == 2 and ex + 1 < E:
                t_st = load_w(ex + 1, tw["w", ex])

        onef = sb("onef", [128, 128], F32)
        CL = sb("CL", [128, 2], F32)
        TAi = sb("TAi", [128, E, 2], I32)
        TAs = sb("TAs", [128, E, 2], I32)
        t_onef = po.do(lambda e: e.memset(onef[:, :], 1.0))

        a = ve.do(lambda e: e.tensor_reduce(BM[:, :], B1[:, :, :], X_AX, ALU.max, apply_absolute_value=True), t_b1)
        a = po.do(lambda e: e.partition_all_reduce(BMA[:, :], BM[:, :], 128, bass.bass_isa.ReduceOp.max), a)
        a = ve.do(lambda e: e.tensor_scalar(eb1[:, :], BMA[:, :].bitcast(I32), 23, None,
                                            ALU.logical_shift_right), a)
        a = ve.do(lambda e: e.tensor_scalar(eb1[:, :], eb1[:, :], 80, 240, ALU.max, ALU.min), a)
        t_eb1 = ve.do(lambda e: e.tensor_scalar(eb1[:, :], eb1[:, :], 1.0, None, ALU.add), a)

        stage_norm(0)
        stage_xn(0)
        pe_xt(0)
        pe_qk(0)
        pe_vg(0)
        pe_tr(0)
        stage_norm(1)
        stage_xn(1)
        t_x[2] = load_x(2)
        for c in range(NC):
            nxt = c + 1 < NC
            if nxt and c > 0:
                stage_xn(c + 1)
            pe_sc(c, 0)
            pe_sc(c, 1)
            if c > 0:
                pe_proj(c - 1)
            pe_sc(c, 2)
            pe_sc(c, 3)
            pe_state(c)
            if nxt:
                pe_xt(c + 1)
            pe_pv(c, 0)
            if nxt:
                pe_qk(c + 1)
            pe_pv(c, 1)
            ss_copy(c)
            pe_den(c)
            if nxt:
                pe_tr(c + 1)
            if nxt:
                pe_vg(c + 1)
            if c + 2 < NC:
                stage_norm(c + 2)
            weights(c)
        pe_proj(NC - 1)

        VA = VB[0]
        R1 = VA[:, 0:256].rearrange("p (c e) -> p c e", e=E)
        R2 = VA[:, 256:512].rearrange("p (c e) -> p c e", e=E)
        O32 = VA[:, 512:768].rearrange("p (c e) -> p c e", e=E)
        TT = VA[:, 768:1024].rearrange("p (e c) -> p e c", e=E)
        PI = VA[:, 1024:1280].rearrange("p (e c) -> p e c", e=E)
        M1 = VA[:, 1280:1312]
        M2 = VA[:, 1312:1344]
        POS = VA[:, 1344:1376]
        POSI = VA[:, 1376:1408].bitcast(I32)
        SLI = VA[:, 1408:1440].bitcast(I32)
        PLI = VA[:, 1440:1472].bitcast(I32)
        NSI = VA[:, 1472:1480].bitcast(I32)
        NSF = VA[:, 1480:1488]
        CSF = VA[:, 1488:1496]
        BAS = VA[:, 1496:1504]
        O16 = VA[:, 1504:1632].bitcast(BF16)
        GE = VB[1][:, 0:NS * 8].rearrange("p (s e) -> p s e", e=8)
        ESF = VB[1][:, 320:320 + NS]
        IDF = VB[1][:, 384:384 + NS]
        EQS = VB[1][:, 512:512 + 32 * NS // 2].bitcast(BF16).rearrange("p (c s) -> p c s", c=32)
        AO = SM[:, :, :].rearrange("p h n -> p (h n)").bitcast(BF16).rearrange("p (c n) -> p c n", c=32)
        BO = QM[:, :, :].rearrange("p h n -> p (h n)").bitcast(BF16)[:, 0:32 * 2 * NS].rearrange(
            "p (c s) -> p c s", c=32)
        wt = cc(C_WT, 8).rearrange("p (o e) -> p o e", o=1).broadcast_to((128, NC, E))

        def bc(ap, n):
            return ap.rearrange("p (c o) -> p c o", o=1).broadcast_to((128, ap.shape[1], n))

        def bm(ap, n):
            return ap.rearrange("p (o c) -> p o c", o=1).broadcast_to((128, n, ap.shape[1]))

        LC = VA[:, 1632:2048]
        t_lc = sp.dma(lambda e: e.dma_start(LC, cst2), slot("k_lc"), g("ppv", NC - 2), g("pst", NC - 2))
        fence = (g("ppv", NC - 1), g("y", NC - 1), g("lg", NC - 1), g("pst", NC - 1))
        a = ve.do(lambda e: e.tensor_tensor(R1, L[:, :, :], bm(GBE[:, 1, :], NC), ALU.add), *fence)
        a = ve.do(lambda e: e.tensor_reduce(M1, R1, X_AX, ALU.max), a)
        a = ve.do(lambda e: e.tensor_tensor(R2, R1, bc(M1, E), ALU.is_equal), a)
        a = ve.do(lambda e: e.tensor_tensor(R2, R2, wt, ALU.mult), a)
        a = ve.do(lambda e: e.tensor_reduce(M2, R2, X_AX, ALU.max), a)
        a = ve.do(lambda e: e.tensor_tensor(O32, bc(M2, E), wt, ALU.is_equal), a)
        a = ve.do(lambda e: e.tensor_copy(O16, VA[:, 512:768]), a)
        pe.do(lambda e: e.matmul(PS[0][:, 0:256], tri16[:, :], O16, start=True, stop=True), a, t_tri, sig=False)
        b = pe.do(lambda e: e.matmul(PS[0][:, 256:512], one16[:, :], O16, start=True, stop=True), t_one)
        a = ve.do(lambda e: e.tensor_copy(TT, PS[0][:, 256:512].rearrange("p (c e) -> p e c", e=E)), b)
        a = ve.do(lambda e: e.tensor_tensor_scan(VA[:, 1024:1280], LC[:, D_RST:D_RST + 256], VA[:, 768:1024], 0.0,
                                                 ALU.mult, ALU.add), a, t_lc)
        a = ve.do(lambda e: e.tensor_scalar(NSI, PI[:, :, NC - 1], 127.0, None, ALU.add), a)
        a = ve.do(lambda e: e.tensor_scalar(NSI, NSI, 7, None, ALU.logical_shift_right), a)
        a = ve.do(lambda e: e.tensor_copy(NSF, NSI), a)
        a = ve.do(lambda e: e.tensor_tensor_scan(CSF, onef[:, 0:8], NSF, 0.0, ALU.mult, ALU.add), a)
        a = ve.do(lambda e: e.tensor_tensor(BAS, CSF, NSF, ALU.subtract), a)
        a = ve.do(lambda e: e.tensor_scalar(BAS, BAS, 128.0, None, ALU.mult), a)
        b = ve.do(lambda e: e.tensor_tensor(GE, bc(cc(C_SL, NS), 8), bm(CSF, NS), ALU.is_ge), a)
        b = ve.do(lambda e: e.tensor_reduce(ESF, GE[:, :, 0:7], X_AX, ALU.add), b)
        t_es = ve.do(lambda e: e.tensor_copy(es[:, :], ESF), b)
        a = ve.do(lambda e: e.tensor_tensor(PI, PI, TT, ALU.subtract))
        a = ve.do(lambda e: e.tensor_tensor(PI, PI, bc(BAS, NC), ALU.add), a)
        a = ve.do(lambda e: e.tensor_tensor(R1, PS[0][:, 0:256].rearrange("p (c e) -> p c e", e=E),
                                            VA[:, 1024:1280].rearrange("p (e c) -> p c e", e=E), ALU.add), a)
        a = ve.do(lambda e: e.tensor_tensor(R1, R1, O32, ALU.mult), a)
        a = ve.do(lambda e: e.tensor_reduce(POS, R1, X_AX, ALU.add), a)
        a = ve.do(lambda e: e.tensor_copy(POSI, POS), a)
        ve.do(lambda e: e.tensor_scalar(SLI, POSI, 7, None, ALU.logical_shift_right), a)
        a = ve.do(lambda e: e.tensor_scalar(PLI, POSI, 127, None, ALU.bitwise_and), a)
        a = ve.do(lambda e: e.tensor_copy(M1, SLI), a)
        a = ve.do(lambda e: e.tensor_copy(M2, PLI), a)
        a = ve.do(lambda e: e.tensor_tensor(EQS, bm(cc(C_SL, NS), NC), bc(M1, NS), ALU.is_equal), a)
        a1 = ve.do(lambda e: e.tensor_tensor(AO, bm(LC[:, D_P:D_P + 128], NC), bc(M2, 128), ALU.is_equal),
                   g("psc", NC - 1))
        ve.do(lambda e: e.tensor_scalar(BO[:, :, 0:NS], EQS, cc(C_T, 1), None, ALU.mult), a)
        a = ve.do(lambda e: e.tensor_tensor(BO[:, :, NS:2 * NS], EQS, bc(LC[:, D_C32:D_C32 + 32], NS), ALU.mult), a)
        for c in range(NC):
            b = pe.do(lambda e, c=c: e.matmul(PS[1][:, 0:2 * NS], AO[:, c, :], BO[:, c, :],
                                              start=(c == 0), stop=(c == NC - 1)), a, sig=(c == NC - 1))
        a = ve.do(lambda e: e.tensor_scalar(IDF, PS[1][:, NS:2 * NS], 128.0, 4096.0, ALU.mult, ALU.add), b)
        a = ve.do(lambda e: e.tensor_tensor(IDF, IDF, PS[1][:, 0:NS], ALU.add), a)
        t_ids = ve.do(lambda e: e.tensor_copy(ids[:, :], IDF), a)

        NG = 4
        Qf = QM[:, :, :].rearrange("p h n -> p (h n)")
        Sf = SM[:, :, :].rearrange("p h n -> p (h n)")
        XG = [Qf[:, i * 512:(i + 1) * 512] for i in range(4)]
        X16 = [Sf[:, i * 256:(i + 1) * 256].bitcast(F16) for i in range(2)]
        XT16 = [Sf[:, 512 + i * 256:768 + i * 256].bitcast(F16) for i in range(2)]
        OUT = [Sf[:, 1024 + i * 256:1280 + i * 256] for i in range(3)]
        RB = [VB[1][:, i * 256:(i + 1) * 256] for i in range(3)]
        H32 = [ST[:, i * 1024:(i + 1) * 1024] for i in range(2)]
        HH = [ST[:, 2048 + i * 512:2560 + i * 512].bitcast(F16) for i in range(2)]
        HL = [ST[:, 3072 + i * 512:3584 + i * 512].bitcast(F16) for i in range(2)]
        B2 = VB[0]
        k_b2 = slot("k_b2")
        k_g = [slot(f"k_g{i}") for i in range(4)]
        k_o = [slot(f"k_o{i}") for i in range(3)]
        t_b2 = sp.dma(lambda e: e.dma_start(B2[:, :], b2), k_b2, t_ids)
        t_z = []
        for i in range(4):
            t_z.append(ve.do(lambda e, i=i: e.memset(XG[i], 0.0), b))
        t_w = tw["w", E - 1]
        reg = {}
        scr_done = tuple(g("st", c) for c in range(NC - 3, NC))

        def gather(s):
            tk["g", s] = po.dma(lambda e: e.indirect_dma_start(
                XG[s % NG], None, scr, bass.IndirectOffsetOnAxis(ids[:, s:s + 1], 0),
                bounds_check=NT - 1, oob_is_err=False), k_g[s % NG],
                t_ids, t_z[s % NG], *scr_done, g("xs", s - NG), g("rb", s - NG))

        def split_x(s):
            xg, x16 = XG[s % NG], X16[s % 2]
            a = ac.do(lambda e: e.activation(x16[:, 0:256], xg[:, 0:256], ACT.Copy, scale=float(2 ** XSH)),
                      g("g", s), g("ptx", s - 2))
            tk["xs", s] = ve.do(lambda e: e.scalar_tensor_tensor(
                x16[:, 256:512], xg[:, 0:256], float(2 ** XSH), x16[:, 0:256], ALU.mult, ALU.subtract), a)

            def addb(e):
                r = e.value_load(es[0:1, s:s + 1], min_val=0, max_val=E - 1)
                reg["ve"] = r
                return e.tensor_tensor(RB[s % 3], xg[:, 256:512], B2[:, bass.ds(r * 256, 256)], ALU.add)

            tk["rb", s] = ve.do(addb, t_b2, t_es, g("g", s), g("o", s - 3))

        def pe_tx(s):
            pt = PS[6][:, 0:256].bitcast(F16)
            for i in range(4):
                a = pe.do(lambda e, i=i: e.transpose(pt[:, i * 128:(i + 1) * 128],
                                                     X16[s % 2][:, i * 128:(i + 1) * 128], id16[:, :]),
                          t_id16, g("xs", s), g("tx", s - 1), sig=(i == 3))
            tk["ptx", s] = a
            tk["tx", s] = ac.do(lambda e: e.activation(XT16[s % 2], pt, ACT.Copy), a, g("pg1", s - 2))

        def pe_g1(s):
            xt = XT16[s % 2]

            def first(e):
                r = e.value_load(es[0:1, s:s + 1], min_val=0, max_val=E - 1)
                reg["pe", s] = r * 8192

            pe.wait(t_es)
            pe.items.append(first)
            ac.wait(t_es)

            def loada(e):
                reg["ac", s] = e.value_load(es[0:1, s:s + 1], min_val=0, max_val=E - 1)

            ac.items.append(loada)
            for f in range(8):
                bank = PS[2 * (s % 2) + f // 4]
                dst = bank[:, (f % 4) * 128:(f % 4 + 1) * 128]
                n = 0
                for k in range(2):
                    for wl, xl in ((0, 0), (0, 1), (1, 0)):
                        n += 1
                        off = wl * 2048 + k * 1024 + f * 128
                        a = pe.do(lambda e, off=off, xl=xl, k=k, n=n, dst=dst: e.matmul(
                            dst, W[:, bass.ds(reg["pe", s] + off, 128)],
                            xt[:, xl * 256 + k * 128:xl * 256 + (k + 1) * 128], start=(n == 1), stop=(n == 6)),
                            g("tx", s), t_w, g("hr", (s - 2, 7)) if f // 4 else g("hr", (s - 2, 3)),
                            sig=(n == 6 and f % 4 == 3))
                if f % 4 == 3:
                    for ff in range(f - 3, f + 1):
                        src = bank[:, (ff % 4) * 128:(ff % 4 + 1) * 128]
                        tk["hr", (s, ff)] = ac.do(lambda e, ff=ff, src=src: e.activation(
                            H32[s % 2][:, ff * 128:(ff + 1) * 128], src, ACT.Relu,
                            bias=B1S[:, bass.ds(reg["ac", s] * 8 + ff, 1)],
                            scale=TAs[:, :, 0][:, bass.ds(reg["ac", s], 1)].bitcast(F32)),
                            a, g("hl", (s - 2, f // 4)), sig=(ff % 4 == 3))
                    q = f // 4
                    sl = slice(q * 512, (q + 1) * 512)
                    t = ve.do(lambda e, sl=sl: e.tensor_copy(HH[s % 2][:, sl], H32[s % 2][:, sl]),
                              tk["hr", (s, f)], g("pg2", s - 2))
                    tk["hl", (s, q)] = ve.do(lambda e, sl=sl: e.tensor_tensor(
                        HL[s % 2][:, sl], H32[s % 2][:, sl], HH[s % 2][:, sl], ALU.subtract), t)
            tk["pg1", s] = a

        def pe_g2(s):
            bank = PS[4 + s % 2]
            n = 0
            for f in range(8):
                for hl, wl in ((0, 0), (0, 1), (1, 0)):
                    n += 1
                    off = 4096 + wl * 2048 + f * 256
                    src = (HL if hl else HH)[s % 2][:, f * 128:(f + 1) * 128]
                    a = pe.do(lambda e, off=off, src=src, n=n: e.matmul(
                        bank[:, 0:256], src, W[:, bass.ds(reg["pe", s] + off, 256)],
                        start=(n == 1), stop=(n == 24)),
                        g("hl", (s, f // 4)), g("o", s - 2), sig=(n == 24))
            tk["pg2", s] = a

            def last(e):
                r = e.value_load(es[0:1, s:s + 1], min_val=0, max_val=E - 1)
                return e.scalar_tensor_tensor(
                    OUT[s % 3], bank[:, 0:256], TAs[:, :, 1][:, bass.ds(r, 1)].bitcast(F32), RB[s % 3],
                    ALU.mult, ALU.add)

            tk["o", s] = ve.do(last, a, g("rb", s), g("sc", s - 3))
            tk["sc", s] = po.dma(lambda e: e.indirect_dma_start(
                outr, bass.IndirectOffsetOnAxis(ids[:, s:s + 1], 0), OUT[s % 3], None,
                bounds_check=NT - 1, oob_is_err=False), k_o[s % 3], tk["o", s])

        gather(0)
        gather(1)
        gather(2)
        split_x(0)
        pe_tx(0)
        split_x(1)
        pe_g1(0)
        pe_tx(1)
        for s in range(NS):
            if s + 3 < NS:
                gather(s + 3)
            if s + 2 < NS:
                split_x(s + 2)
            if s + 1 < NS:
                pe_g1(s + 1)
            if s + 2 < NS:
                pe_tx(s + 2)
            pe_g2(s)
        po.wait(*(g("sc", s) for s in range(NS - 3, NS)))

        block = ctx.enter_context(nc.Block())
        block.tensor(pe.run)
        block.vector(ve.run)
        block.scalar(ac.run)
        block.gpsimd(po.run)
        block.sync(sp.run)


def kernel(**inputs):
    import numpy as np
    import concourse.bacc as _bacc
    from concourse import mybir as _mybir
    from concourse.bass_utils import run_bass_kernel_spmd as _run

    p = "L0_ffn_"
    x = np.ascontiguousarray(inputs["L0_attn_x"])
    wall = np.concatenate([inputs["L0_attn_w_attn"], inputs[p + "gate_w"]], 0)
    wall = np.ascontiguousarray(wall.T.reshape(2, 128, 776).transpose(1, 0, 2))
    wp = np.ascontiguousarray(np.asarray(inputs["L0_attn_w_proj"]).T.reshape(2, 128, 256).transpose(1, 0, 2))
    gb = np.ascontiguousarray(np.broadcast_to(np.asarray(inputs[p + "gate_b"])[None], (128, E)))
    eb = np.ascontiguousarray(np.broadcast_to(np.asarray(inputs[p + "expert_bias"])[None], (128, E)))
    w1 = np.ascontiguousarray(np.asarray(inputs[p + "w1"]).reshape(E, 2, 128, F).transpose(0, 2, 1, 3)
                              .reshape(E, 128, 2048))
    w2 = np.ascontiguousarray(np.asarray(inputs[p + "w2"]).reshape(E, 8, 128, D).transpose(0, 2, 1, 3)
                              .reshape(E, 128, 2048))
    b1 = np.ascontiguousarray(np.asarray(inputs[p + "b1"]).reshape(E, 8, 128).transpose(2, 0, 1))
    b2 = np.ascontiguousarray(np.broadcast_to(np.asarray(inputs[p + "b2"]).reshape(1, E * D), (128, E * D)))

    i = np.arange(128)
    cst = np.zeros((128, C_N), np.float32)
    cst[:, C_ID:C_ID + 128] = np.eye(128)
    cst[:, C_MASK:C_MASK + 128] = i[None, :] >= i[:, None]
    bd = (i[:, None] // 16) == (i[None, :] // 16)
    cst[:, C_BD:C_BD + 128] = bd
    cst[:, C_HM:C_HM + 8] = (i[:, None] // 16) == np.arange(8)[None]
    cst[:, C_WT:C_WT + 8] = 8 - np.arange(8)[None]
    cst[:, C_SL:C_SL + NS] = np.arange(NS)[None]
    cst2 = np.zeros((128, D_N), np.float32)
    cst2[:, D_P:D_P + 128] = i[None]
    cst2[:, D_C32:D_C32 + 32] = np.arange(32)[None] - 32
    cst2[:, D_RST:D_RST + 256] = (np.arange(256) % 32 != 0)[None]
    tri = (i[:, None] < i[None, :]).astype(np.float32)
    cst[:, C_T] = i

    nc = _bacc.Bacc("TRN2", target_bir_lowering=False, num_devices=1)
    arrays, args = {}, []
    for name, a in (("x", x), ("wall", wall), ("wp", wp), ("gb", gb), ("eb", eb), ("w1", w1), ("b1", b1),
                    ("w2", w2), ("b2", b2), ("cst", cst), ("cst2", cst2), ("tri", tri)):
        arrays[f"in_{name}"] = a
        args.append(nc.dram_tensor(f"in_{name}", a.shape, _mybir.dt.from_np(a.dtype), kind="ExternalInput").ap())
    args.append(nc.dram_tensor("out_0", (B, T, D), _mybir.dt.float32, kind="ExternalOutput").ap())
    program(nc, *args)
    r = _run(nc, [arrays], core_ids=[0])
    return r.results[0]["out_0"]
```

```python
from contextlib import ExitStack

import concourse.bass as bass
from concourse import mybir

F32 = mybir.dt.float32
F16 = mybir.dt.float16
BF16 = mybir.dt.bfloat16
I32 = mybir.dt.int32
ALU = mybir.AluOpType
ACT = mybir.ActivationFunctionType
X_AX = mybir.AxisListType.X

B, T, D = 4, 1024, 256
NT = B * T
NC = NT // 128
CPB = T // 128
H = 16
E = 8
F = 1024
NS = NT // 128 + E - 1
XSH = 10
R = 8

C_ID, C_MASK, C_PM, C_ONE, C_WT, C_SL, C_T, C_N = (0, 128, 256, 290, 298, 306, 345, 346)
D_RST, D_P, D_C32, D_N = (0, 256, 384, 416)


PERIOD = 12.1
STEPS = dict(
    na=0.12, nn=0.13, wa0=3.87, wd0=4.65, wa1=6.30, wd1=8.55, wa2=11.97, wd2=12.65, wa3=13.58,
    nb=13.85, wd3=14.89, xh=14.96, xl=15.84, xt=15.85, xTc=17.17, qk=18.17, relu=20.79, exp=21.94,
    vg=23.92, phi=24.54, hq=24.55, hk=24.87, lq=24.89, vh=25.11, lk=25.12, cq=25.25, ck=25.36,
    vl=25.66, trq=25.74, trk=25.81, st=26.30, kz=26.44, qs=26.88, sc0=26.89, s1=27.03, s0=27.06,
    sh1=28.16, t32=28.51, sh0=29.44, sc2=29.63, sl1=29.65, s3=30.18, sl0=30.26, sh3=31.66,
    inter=32.84, pv0=32.85, pv1=32.86, s2=33.37, sl3=33.45, sh2=33.58, sl2=33.59, lg=36.01,
    pv2=36.69, pv3=36.71, y=37.40, t0=37.65, yh=37.98, yl=37.99, yt=38.49, t1=38.53, yTc=39.26,
    t1a=39.31, pr=39.44, t2=40.06, res=40.23)


class Engine:

    def __init__(self, sem):
        self.sem, self.count, self.items, self.seen = sem, 0, [], {}

    def wait(self, *tokens):
        for t in tokens:
            if t is None:
                continue
            sem, v = t
            if self.seen.get(id(sem), 0) < v:
                self.seen[id(sem)] = v
                self.items.append(lambda e, sem=sem, v=v: e.wait_ge(sem, v))

    def do(self, fn, *tokens, sig=True):
        self.wait(*tokens)
        if sig:
            self.count += 1
            self.items.append(lambda e: fn(e).then_inc(self.sem, 1))
            return (self.sem, self.count)
        self.items.append(fn)
        return None

    def dma(self, fn, slot, *tokens):
        self.wait(*tokens)
        slot.count += 16
        self.items.append(lambda e: fn(e).then_inc(slot.sem, 16))
        return (slot.sem, slot.count)

    def run(self, e):
        for f in self.items:
            f(e)


class Slot:

    def __init__(self, sem):
        self.sem, self.count = sem, 0


def program(nc, x, wall, wp, gb, eb, w1, b1, w2, b2, cst, cst2, tri, out):
    ctx = ExitStack()
    with ctx:
        def sb(name, shape, dt):
            return ctx.enter_context(nc.sbuf_tensor(name, shape, dt))

        def sem(name):
            return ctx.enter_context(nc.semaphore(name))

        def slot(name):
            return Slot(sem(name))

        PS = [ctx.enter_context(nc.psum_tensor(f"ps{i}", [128, 512], F32)) for i in range(8)]

        W = sb("W", [128, E * 8192], F16)
        ST = sb("ST", [128, 4096], F32)
        CT = sb("CT", [128, C_N], F32)
        XR = [sb(f"XR{i}", [128, 512], F32) for i in range(R - 1)]
        xT = [sb(f"xT{i}", [128, 512], F16) for i in range(2)]
        WA = sb("WA", [128, 2, 2, 776], F16)
        WP = sb("WP", [128, 2, 2, 256], F16)
        AR = sb("AR", [128, 7968], F32)
        T32 = sb("T32", [128, 272], F32)
        T16 = sb("T16", [128, 3, 272], BF16)
        L = sb("L", [128, NC, E], F32)
        GBE = sb("GBE", [128, 2, E], F32)
        st6 = sb("st6", [128, 6], F32)
        mv = sb("mv", [128, 4, 2], F32)
        rsn = sb("rsn", [128, 2, 4, 2], F32)
        nv = sb("nv", [128, 4], F32)
        nr = sb("nr", [128, 2], F32)
        nvi = sb("nvi", [128, 1], I32)
        DN = sb("DN", [128, 16], F32)
        tri16 = sb("tri16", [128, 128], BF16)
        one16 = sb("one16", [128, 128], BF16)
        id16 = sb("id16", [128, 128], F16)
        B1 = sb("B1", [128, E, 8], F32)
        B1S = sb("B1S", [128, E * 8], F32)
        MX4 = sb("MX4", [128, 2, 4], F32)
        MX = sb("MX", [128, E, 2], F32)
        MXA = sb("MXA", [128, E, 2], F32)
        BM = sb("BM", [128, E], F32)
        BMA = sb("BMA", [128, E], F32)
        ea = sb("ea", [128, E, 2], I32)
        eb1 = sb("eb1", [128, E], I32)
        Eh = sb("Eh", [128, E], I32)
        ti = sb("ti", [128, E, 4], I32)
        SC = sb("SC", [128, E, 4], I32)
        TAi = sb("TAi", [128, E, 2], I32)
        TAs = sb("TAs", [128, E, 2], I32)
        ni = sb("ni", [128, 4], I32)
        nw = sb("nw", [128, 2], F32)
        SI = sb("SI", [128, 8], I32)
        SV = sb("SV", [128, 8], I32)
        EP = sb("EP", [128, 1], F32)
        es = sb("es", [128, NS], I32)
        ids = sb("ids", [128, NS], I32)

        def ar(a, n, dt=F32):
            v = AR[:, a:a + n]
            return v if dt == F32 else v.bitcast(dt)

        KT = ar(0, 512, F16).rearrange("p (j n) -> p j n", j=8)
        XR.append(ar(512, 512))
        QS = ar(1024, 512, F16).rearrange("p (j n) -> p j n", j=8)
        SH = ar(1536, 1024, F16).rearrange("p (h n) -> p h n", h=16)
        SL = ar(2560, 1024, F16).rearrange("p (h n) -> p h n", h=16)
        S32 = [ar(3584 + 512 * i, 512) for i in range(2)]
        QK = ar(4608, 512)
        P16 = ar(6944, 1024, F16)
        V16 = [ar(5632 + 272 * i, 272, F16).rearrange("p (l h e) -> p l h e", l=2, h=16) for i in range(2)]
        Y32 = ar(6176, 256)
        Y16 = ar(6432, 256, F16)
        yT = ar(6688, 256, F16)
        X16 = ar(5120, 256, F16)

        scr = nc.dram_tensor("scr", [NT, 512], F32, kind="Internal").ap()
        outr = out.rearrange("b t d -> (b t) d")
        xr = x.rearrange("b t d -> (b t) d")

        pe, ve, ac, po, sp = (Engine(sem(n)) for n in ("s_pe", "s_ve", "s_ac", "s_po", "s_sp"))

        def cc(a, n, p=128):
            return CT[0:p, a:a + n]

        k_ct, k_wa, k_wp, k_sm = slot("k_ct"), slot("k_wa"), slot("k_wp"), slot("k_sm")
        k_x = [slot(f"k_x{i}") for i in range(R)]
        k_st = [slot("k_st0"), slot("k_st1")]
        k_scr = [slot(f"k_scr{i}") for i in range(R)]

        def load_x(c):
            return sp.dma(lambda e: e.dma_start(XR[c % R][:, 256:512], xr[c * 128:(c + 1) * 128, :]),
                          k_x[c % R], *t_free.get(c, ()))

        t_free = {}
        t_x = {}
        WF = ar(0, 1552).rearrange("p (k n) -> p k n", k=2)
        WPF = ar(1552, 512).rearrange("p (k n) -> p k n", k=2)
        SQ = ar(2064, 1552).rearrange("p (k n) -> p k n", k=2)
        SQP = ar(3616, 512).rearrange("p (k n) -> p k n", k=2)
        TRI = ar(4128, 128)
        ONF = ar(4256, 128)
        t_x[0] = load_x(0)
        t_wa = sp.dma(lambda e: e.dma_start(WF, wall), k_wa)
        t_ct = sp.dma(lambda e: e.dma_start(CT[:, :], cst), k_ct)
        t_x[1] = load_x(1)
        t_wp = sp.dma(lambda e: e.dma_start(WPF, wp), k_wp)
        t_tr = sp.dma(lambda e: e.dma_start(TRI, tri), slot("k_tri"))
        sp.dma(lambda e: e.dma_start(GBE[:, 0, :], gb), k_sm)
        sp.dma(lambda e: e.dma_start(GBE[:, 1, :], eb), k_sm)
        t_b1 = sp.dma(lambda e: e.dma_start(B1[:, :, :], b1), k_sm)

        def load_w(ex, i, *tokens):
            return sp.dma(lambda e: e.dma_start(ST[:, i * 2048:(i + 1) * 2048], (w1, w2)[i][ex]),
                          k_st[i], *tokens)

        t_st = [load_w(0, 0), load_w(0, 1)]

        t_onef = po.do(lambda e: e.memset(ONF, 1.0))
        t_id16 = po.do(lambda e: e.tensor_copy(id16[:, :], cc(C_ID, 128)), t_ct)
        t_one = po.do(lambda e: e.memset(one16[:, :], 1.0))
        t_tri = po.do(lambda e: e.tensor_copy(tri16[:, :], TRI), t_tr)
        for i in range(2):
            po.do(lambda e, i=i: e.memset(V16[i][:, 0, :, 16:17], 1.0))
            t_v1 = po.do(lambda e, i=i: e.memset(V16[i][:, 1, :, 16:17], 0.0))

        a = ve.do(lambda e: e.tensor_tensor(SQ, WF, WF, ALU.mult), t_wa)
        b = ve.do(lambda e: e.tensor_tensor(SQP, WPF, WPF, ALU.mult), t_wp)
        for n0, n1, bank in ((0, 512, 0), (512, 776, 1)):
            for k in range(2):
                pe.do(lambda e, k=k, n0=n0, n1=n1, bank=bank: e.matmul(
                    PS[bank][:, 0:n1 - n0], ONF, SQ[:, k, n0:n1], start=(k == 0), stop=(k == 1)),
                    a, t_onef, sig=False)
        for k in range(2):
            a = pe.do(lambda e, k=k: e.matmul(PS[2][:, 0:256], ONF, SQP[:, k, :], start=(k == 0), stop=(k == 1)),
                      b, sig=(k == 1))
        ve.do(lambda e: e.tensor_reduce(nv[:, 0:1], PS[0][:, :], X_AX, ALU.max), a)
        a1 = ve.do(lambda e: e.tensor_reduce(nv[:, 1:2], PS[1][:, 0:264], X_AX, ALU.max), a)
        ve.do(lambda e: e.tensor_reduce(nw[:, 1:2], PS[2][:, 0:256], X_AX, ALU.max), a)
        a = ve.do(lambda e: e.tensor_tensor(nw[:, 0:1], nv[:, 0:1], nv[:, 1:2], ALU.max), a1)
        a = ve.do(lambda e: e.tensor_scalar(ni[:, 0:2], nw[:, :].bitcast(I32), 23, None,
                                            ALU.logical_shift_right), a)
        a = ve.do(lambda e: e.tensor_scalar(ni[:, 0:2], ni[:, 0:2], 20, 240, ALU.max, ALU.min), a)
        a = ve.do(lambda e: e.tensor_scalar(ni[:, 0:2], ni[:, 0:2], 1.0, None, ALU.add), a)
        a = ve.do(lambda e: e.tensor_scalar(ni[:, 0:2], ni[:, 0:2], 1, None, ALU.logical_shift_right), a)
        a = ve.do(lambda e: e.tensor_scalar(ni[:, 2:3], ni[:, 0:1], 59, None, ALU.max), a)
        ve.do(lambda e: e.tensor_scalar(SI[:, 0:2], ni[:, 0:2], -1.0, 205.0, ALU.mult, ALU.add), a)
        ve.do(lambda e: e.tensor_scalar(SI[:, 2:3], ni[:, 2:3], -1.0, 200.0, ALU.mult, ALU.add))
        ve.do(lambda e: e.tensor_scalar(SI[:, 3:4], ni[:, 0:1], 39.0, None, ALU.add))
        ve.do(lambda e: e.scalar_tensor_tensor(SI[:, 4:5], ni[:, 0:1], 112.0, ni[:, 2:3], ALU.add, ALU.subtract))
        a = ve.do(lambda e: e.scalar_tensor_tensor(SI[:, 5:6], ni[:, 2:3], -24.0, ni[:, 1:2], ALU.add, ALU.add))
        t_sv = ve.do(lambda e: e.tensor_scalar(SV[:, 0:6], SI[:, 0:6], 23, None, ALU.logical_shift_left), a)

        def sv(i):
            return SV[:, i:i + 1].bitcast(F32)

        a = ve.do(lambda e: e.tensor_scalar(EP[:, :], sv(2), sv(2), 1e-6 * 2.0 ** -19, ALU.mult, ALU.mult), t_sv)
        t_ep = a
        a = ac.do(lambda e: e.activation(WA[:, 0, :, :], WF, ACT.Copy, scale=sv(0)), t_sv)
        t_wah = ve.do(lambda e: e.scalar_tensor_tensor(WA[:, 1, :, :], WF, sv(0), WA[:, 0, :, :],
                                                       ALU.mult, ALU.subtract), a)
        a = ac.do(lambda e: e.activation(WP[:, 0, :, :], WPF, ACT.Copy, scale=sv(1)))
        t_wph = ve.do(lambda e: e.scalar_tensor_tensor(WP[:, 1, :, :], WPF, sv(1), WP[:, 0, :, :],
                                                       ALU.mult, ALU.subtract), a)

        tk = {}

        def g(what, c):
            return tk.get((what, c))

        last = {}

        def put(what, c, token):
            tk[what, c] = last[what] = token
            return token

        def na(c):
            xb, m, r_ = XR[c % R], mv[:, c % 4, :], rsn[:, c // 2 % 2, :, c % 2:c % 2 + 1]
            a = ve.do(lambda e: e.bn_stats(st6[:, :], xb[:, 256:512]), t_x[c])
            a = ve.do(lambda e: e.bn_aggr(m, st6[:, :]), a)
            a = ve.do(lambda e: e.tensor_scalar(r_[:, 1], m[:, 1:2], 1e-5, None, ALU.add), a,
                      g("nn", c - 4 + (c + 1) % 2))
            a = ve.do(lambda e: e.tensor_scalar(r_[:, 2].bitcast(I32), r_[:, 1].bitcast(I32), 1, None,
                                                ALU.logical_shift_right), a)
            put("na", c, ve.do(lambda e: e.tensor_scalar(r_[:, 0].bitcast(I32), r_[:, 2].bitcast(I32), -1.0,
                                                         float(0x5f3759df), ALU.mult, ALU.add), a,
                               g("nb", c - 4)))

        def nn(c):
            if c % 2 == 0:
                return
            r_ = rsn[:, c // 2 % 2, :, :]
            a = g("na", c)
            for k in range(3):
                m = 1.0 if k < 2 else float(2 ** XSH)
                a = po.do(lambda e: e.tensor_tensor(nr[:, :], r_[:, 0], r_[:, 0], ALU.mult), a)
                a = po.do(lambda e: e.tensor_tensor(nr[:, :], nr[:, :], r_[:, 1], ALU.mult), a)
                a = po.do(lambda e, m=m: e.tensor_scalar(nr[:, :], nr[:, :], -0.5 * m, 1.5 * m,
                                                         ALU.mult, ALU.add), a)
                a = po.do(lambda e: e.tensor_tensor(r_[:, 0], r_[:, 0], nr[:, :], ALU.mult), a)
            put("nn", c, a)
            put("nn", c - 1, a)

        def nb(c):
            xb = XR[c % R]
            put("nb", c, ve.do(lambda e: e.tensor_scalar(
                xb[:, 0:256], xb[:, 256:512], mv[:, c % 4, 0:1], rsn[:, c // 2 % 2, 0, c % 2:c % 2 + 1],
                ALU.subtract, ALU.mult), g("nn", c)))

        def xh(c):
            put("xh", c, ac.do(lambda e: e.activation(X16[:, 0:256], XR[c % R][:, 0:256], ACT.Copy),
                               g("nb", c), g("xt", c - 1)))

        def xl(c):
            put("xl", c, po.do(lambda e: e.tensor_tensor(X16[:, 256:512], XR[c % R][:, 0:256], X16[:, 0:256],
                                                         ALU.subtract), g("xh", c)))

        b7 = PS[7][:, :].bitcast(F16)

        def xt(c):
            for i in range(4):
                a = pe.do(lambda e, i=i: e.transpose(b7[:, i * 128:(i + 1) * 128],
                                                     X16[:, i * 128:(i + 1) * 128], id16[:, :]),
                          g("xl", c), t_id16, g("xTc", c - 1), last.get("yTc"), sig=(i == 3))
            put("xt", c, a)

        def xTc(c):
            put("xTc", c, ac.do(lambda e: e.activation(xT[c % 2][:, :], b7[:, 0:512], ACT.Copy),
                                g("xt", c), g("qk", c - 2), g("vg", c - 2)))

        def x_w(c, dst, n0, n1, *tokens):
            n = 0
            for k in range(2):
                for xl_, wl in ((0, 0), (0, 1), (1, 0)):
                    n += 1
                    a = pe.do(lambda e, k=k, xl_=xl_, wl=wl, n=n: e.matmul(
                        dst, xT[c % 2][:, xl_ * 256 + k * 128:xl_ * 256 + (k + 1) * 128], WA[:, wl, k, n0:n1],
                        start=(n == 1), stop=(n == 6)), t_wah, g("xTc", c), *tokens, sig=(n == 6))
            return a

        def qk(c):
            put("qk", c, x_w(c, PS[0][:, :], 0, 512, g("kz", c - 1)))

        def relu(c):
            put("relu", c, ac.do(lambda e: e.activation(QK, PS[0][:, :], ACT.Relu, scale=sv(3)),
                                 g("qk", c), g("lk", c - 1), g("lq", c - 1)))

        def exp(c):
            put("exp", c, ac.do(lambda e: e.activation(PS[0][:, :], PS[0][:, :], ACT.Exp, scale=sv(3)),
                                g("relu", c)))

        def phi(c):
            put("phi", c, ve.do(lambda e: e.scalar_tensor_tensor(QK, PS[0][:, :], 1.0, QK, ALU.min, ALU.add),
                                g("exp", c)))

        qd = P16[:, 0:1024].rearrange("p (a n) -> p a n", a=16)
        kd = P16[:, 1024:2048].rearrange("p (a n) -> p a n", a=16)
        q4 = P16[:, 0:1024].rearrange("p (a u d) -> p a u d", a=32, u=2)
        qv = QK.rearrange("p (a d) -> p a d", a=32)

        def hk(c):
            put("hk", c, ac.do(lambda e: e.activation(kd[:, :, 0:16], qv[:, 16:32], ACT.Copy, scale=sv(2)),
                               g("phi", c), g("trk", c - 1), g("st", c - 1)))

        def lk(c):
            put("lk", c, ve.do(lambda e: e.scalar_tensor_tensor(
                kd[:, :, 16:32], qv[:, 16:32], sv(2), kd[:, :, 0:16], ALU.mult, ALU.subtract), g("hk", c)))

        def ck(c):
            put("ck", c, ve.do(lambda e: e.tensor_copy(kd[:, :, 32:64], kd[:, :, 0:32]), g("lk", c)))

        def hq(c):
            put("hq", c, ac.do(lambda e: e.activation(qd[:, :, 0:16], qv[:, 0:16], ACT.Copy, scale=sv(2)),
                               g("phi", c), g("trq", c - 1)))

        def lq(c):
            put("lq", c, ve.do(lambda e: e.scalar_tensor_tensor(
                qd[:, :, 32:48], qv[:, 0:16], sv(2), qd[:, :, 0:16], ALU.mult, ALU.subtract), g("hq", c)))

        def cq(c):
            put("cq", c, ve.do(lambda e: e.tensor_copy(q4[:, :, 1], q4[:, :, 0]), g("lq", c)))

        pv1_ = PS[1][:, 0:256].rearrange("p (h e) -> p h e", h=16)

        def vg(c):
            put("vg", c, x_w(c, PS[1][:, 0:264], 512, 776, g("lg", c - 1)))

        def vh(c):
            put("vh", c, ac.do(lambda e: e.activation(V16[c % 2][:, 0, :, 0:16], pv1_, ACT.Copy, scale=sv(4)),
                               g("vg", c), t_v1, g("pv", (c - 2, 3)), g("st", c - 2)))

        def vl(c):
            v = V16[c % 2]
            put("vl", c, ve.do(lambda e: e.scalar_tensor_tensor(v[:, 1, :, 0:16], pv1_, sv(4), v[:, 0, :, 0:16],
                                                                ALU.mult, ALU.subtract), g("vh", c)))

        def lg(c):
            put("lg", c, ve.do(lambda e: e.scalar_tensor_tensor(
                L[:, c, :], PS[1][:, 256:264], sv(3), GBE[:, 0, :], ALU.mult, ALU.add), g("vg", c), t_b1))

        b0 = PS[0][:, :].bitcast(F16)
        b2_ = PS[2][:, :].bitcast(F16)

        def trk(c):
            for j in range(8):
                a = pe.do(lambda e, j=j: e.transpose(b0[:, j * 128:(j + 1) * 128],
                                                     P16[:, 1024 + j * 128:1152 + j * 128], id16[:, :]),
                          g("ck", c), sig=(j == 7))
            put("trk", c, a)

        def kz(c):
            put("kz", c, ve.do(lambda e: e.tensor_copy(KT, b0.rearrange("p (j n) -> p j n", j=8)),
                               g("trk", c), g("sc", (c - 1, 3))))

        def trq(c):
            for j in range(8):
                a = pe.do(lambda e, j=j: e.transpose(b2_[:, j * 128:(j + 1) * 128],
                                                     P16[:, j * 128:(j + 1) * 128], id16[:, :]),
                          g("cq", c), last.get("res"), sig=(j == 7))
            put("trq", c, a)

        def qs(c):
            put("qs", c, ac.do(lambda e: e.activation(QS, b2_.rearrange("p (j n) -> p j n", j=8), ACT.Copy),
                               g("trq", c), g("sc", (c - 1, 3)), g("in", c - 1)))

        msk = CT[:, C_MASK:C_MASK + 128].rearrange("p (o n) -> p o n", o=1).broadcast_to((128, 4, 128))

        def before(what, c, i):
            return g(what, (c, i - 2)) if i >= 2 else g(what, (c - 1, i + 2))

        def sc(c, i):
            for q in range(8):
                j, r0 = 2 * i + q // 2, 64 * (q % 2)
                bank = PS[3 + q % 2]
                a = pe.do(lambda e, q=q, j=j, r0=r0, bank=bank: e.matmul(
                    bank[:, (q // 2) * 128:(q // 2 + 1) * 128], KT[r0:r0 + 64, j, :], QS[r0:r0 + 64, j, :],
                    start=True, stop=True), g("kz", c), g("qs", c), before("s", c, i), before("s", c, i + 1),
                    sig=(q >= 6))
                put("sc", (c, i + q % 2), a)

        def s_(c, i):
            bank = PS[3 + i % 2]
            s32 = S32[i % 2].rearrange("p (h n) -> p h n", h=4)
            put("s", (c, i), ve.do(lambda e: e.scalar_tensor_tensor(
                s32, bank[:, :].rearrange("p (h n) -> p h n", h=4), 2.0 ** -19, msk, ALU.mult, ALU.mult),
                g("sc", (c, i)), before("sl", c, i)))

        def sh(c, i):
            s32 = S32[i % 2].rearrange("p (h n) -> p h n", h=4)
            put("sh", (c, i), ac.do(lambda e: e.activation(SH[:, 4 * i:4 * i + 4, :], s32, ACT.Copy),
                                    g("s", (c, i)), g("pv", (c - 1, i))))

        def sl(c, i):
            s32 = S32[i % 2].rearrange("p (h n) -> p h n", h=4)
            put("sl", (c, i), po.do(lambda e: e.tensor_tensor(SL[:, 4 * i:4 * i + 4, :], s32,
                                                              SH[:, 4 * i:4 * i + 4, :], ALU.subtract),
                                    g("sh", (c, i))))

        PV = PS[5]

        def inter(c):
            if c % CPB == 0:
                return
            for j in range(8):
                for p in range(3):
                    a = pe.do(lambda e, j=j, p=p: e.matmul(
                        PV[:, j * 34:(j + 1) * 34], QS[:, j, :], T16[:, p, j * 34:(j + 1) * 34],
                        start=(j == 0 and p == 0), stop=True, skip_group_check=True),
                        g("qs", c), g("t2", c - 1), g("y", c - 1), sig=(j == 7 and p == 2))
            put("in", c, a)

        def pv(c, i):
            v = V16[c % 2]
            for b in range(4):
                h = 8 * (i // 2) + 2 * b + i % 2
                dst = PV[:, h * 17:(h + 1) * 17]
                for n, (sp_, l) in enumerate(((SH, 0), (SH, 1), (SL, 0))):
                    a = pe.do(lambda e, h=h, b=b, sp_=sp_, l=l, n=n, dst=dst: e.matmul(
                        dst, sp_[:, 4 * i + b, :], v[:, l, h, :],
                        start=(c % CPB == 0 and i == 0 and b == 0 and n == 0), stop=True, skip_group_check=True),
                        g("vl", c), g("sl", (c, i)), g("y", c - 1), sig=(b == 3 and n == 2))
            put("pv", (c, i), a)

        def y(c):
            o = PV[:, 0:272].rearrange("p (h e) -> p h e", h=16)
            d = DN[:, :].rearrange("p (h o) -> p h o", o=1)
            b = ve.do(lambda e: e.tensor_scalar(d, o[:, :, 16:17], EP[:, 0:1], None, ALU.add),
                      g("pv", (c, 3)), t_ep)
            b = ve.do(lambda e: e.reciprocal(DN[:, :], DN[:, :]), b)
            yv = Y32.rearrange("p (h e) -> p h e", h=16)
            put("y", c, ve.do(lambda e: e.tensor_tensor(yv, o[:, :, 0:16], d.broadcast_to((128, 16, 16)),
                                                        ALU.mult), b, g("yl", c - 1)))

        def yh(c):
            put("yh", c, ac.do(lambda e: e.activation(Y16[:, 0:256], Y32, ACT.Copy), g("y", c), g("yt", c - 1)))

        def yl(c):
            put("yl", c, po.do(lambda e: e.tensor_tensor(Y16[:, 256:512], Y32, Y16[:, 0:256], ALU.subtract),
                               g("yh", c)))

        def yt(c):
            for i in range(4):
                a = pe.do(lambda e, i=i: e.transpose(b7[:, 512 + i * 128:512 + (i + 1) * 128],
                                                     Y16[:, i * 128:(i + 1) * 128], id16[:, :]),
                          g("yl", c), last.get("xTc"), sig=(i == 3))
            put("yt", c, a)

        def yTc(c):
            put("yTc", c, ac.do(lambda e: e.activation(yT, b7[:, 512:1024], ACT.Copy), g("yt", c),
                                g("pr", c - 1)))

        def pr(c):
            n = 0
            for k in range(2):
                for yl_, wl in ((0, 0), (0, 1), (1, 0)):
                    n += 1
                    a = pe.do(lambda e, k=k, yl_=yl_, wl=wl, n=n: e.matmul(
                        PS[2][:, 0:256], yT[:, yl_ * 256 + k * 128:yl_ * 256 + (k + 1) * 128], WP[:, wl, k, :],
                        start=(n == 1), stop=(n == 6)), t_wph, g("yTc", c), last.get("qs"), sig=(n == 6))
            put("pr", c, a)

        def res(c):
            xb = XR[c % R]
            put("res", c, ve.do(lambda e: e.scalar_tensor_tensor(
                xb[:, 256:512], PS[2][:, 0:256], sv(5), xb[:, 256:512], ALU.mult, ALU.add), g("pr", c)))
            tk["str", c] = sp.dma(lambda e: e.dma_start(scr[c * 128:(c + 1) * 128, :], xb[:, :]),
                                  k_scr[c % R], tk["res", c])
            t_free[c + R] = (tk["str", c],)
            if c + R < NC:
                t_x[c + R] = load_x(c + R)

        def st(c):
            if c % CPB == CPB - 1:
                return
            v = V16[c % 2]
            for j in range(8):
                for l in range(2):
                    a = pe.do(lambda e, j=j, l=l: e.matmul(
                        PS[6][:, j * 34:(j + 1) * 34], P16[:, 1024 + j * 128:1152 + j * 128],
                        v[:, l, 2 * j:2 * j + 2, :],
                        start=(c % CPB == 0 and j == 0 and l == 0), stop=True, skip_group_check=True),
                        g("vl", c), g("ck", c), last.get("t32"), sig=(j == 7 and l == 1))
            put("st", c, a)

        t4 = T32[:, :].rearrange("p (j n) -> p j n", j=8)
        mm = CT[:, C_PM:C_PM + 34].rearrange("p (o n) -> p o n", o=1).broadcast_to((128, 8, 34))

        def t32(c):
            put("t32", c, ve.do(lambda e: e.scalar_tensor_tensor(
                t4, PS[6][:, 0:272].rearrange("p (j n) -> p j n", j=8), 2.0 ** -19, mm, ALU.mult, ALU.mult),
                g("st", c), last.get("t2")))

        def t0(c):
            put("t0", c, ac.do(lambda e: e.activation(T16[:, 0, :], T32[:, :], ACT.Copy), g("t32", c),
                               g("in", c), g("in", c - 1)))

        def t1(c):
            put("t1", c, po.do(lambda e: e.tensor_tensor(T32[:, :], T32[:, :], T16[:, 0, :], ALU.subtract),
                               g("t0", c)))

        def t1a(c):
            put("t1a", c, ac.do(lambda e: e.activation(T16[:, 1, :], T32[:, :], ACT.Copy), g("t1", c)))

        def t2(c):
            put("t2", c, po.do(lambda e: e.tensor_tensor(T16[:, 2, :], T32[:, :], T16[:, 1, :], ALU.subtract),
                               g("t1a", c)))

        tw = {}
        small = []

        def w_max(ex, i, q):
            tw["mx", i, q] = ve.do(lambda e: e.tensor_reduce(
                MX4[:, i, q:q + 1], ST[:, i * 2048 + q * 512:i * 2048 + (q + 1) * 512], X_AX, ALU.max,
                apply_absolute_value=True), t_st[i])

        def w_scales(ex):
            a = ve.do(lambda e: e.tensor_reduce(MX[:, ex, :], MX4[:, :, :], X_AX, ALU.max), tw["mx", 1, 3])
            t = [po.do(lambda e: e.partition_all_reduce(
                MXA[:, ex, :], MX[:, ex, :], 128, bass.bass_isa.ReduceOp.max), a)]

            def step(fn, *tokens):
                def run():
                    t[0] = tw["sc"] = ve.do(fn, t[0], *tokens)
                small.append(run)

            step(lambda e: e.tensor_scalar(ea[:, ex, :], MXA[:, ex, :].bitcast(I32), 23, None,
                                           ALU.logical_shift_right))
            step(lambda e: e.tensor_scalar(ea[:, ex, :], ea[:, ex, :], 80, 240, ALU.max, ALU.min))
            step(lambda e: e.scalar_tensor_tensor(
                Eh[:, ex:ex + 1], ea[:, ex, 0:1], 9.0, eb1[:, ex:ex + 1], ALU.add, ALU.max), t_eb1)
            step(lambda e: e.tensor_scalar(ti[:, ex, 0:2], ea[:, ex, :], -1.0, 268.0, ALU.mult, ALU.add))
            step(lambda e: e.tensor_scalar(ti[:, ex, 2:3], Eh[:, ex:ex + 1], -1.0, 268.0, ALU.mult, ALU.add))
            step(lambda e: e.scalar_tensor_tensor(
                TAi[:, ex, 0:1], ea[:, ex, 0:1], 117.0, Eh[:, ex:ex + 1], ALU.add, ALU.subtract))
            step(lambda e: e.scalar_tensor_tensor(
                TAi[:, ex, 1:2], ea[:, ex, 1:2], -155.0, Eh[:, ex:ex + 1], ALU.add, ALU.add))
            step(lambda e: e.tensor_scalar(TAi[:, ex, :], TAi[:, ex, :], 1, 254, ALU.max, ALU.min))
            step(lambda e: e.tensor_scalar(SC[:, ex, 0:3], ti[:, ex, 0:3], 23, None, ALU.logical_shift_left))
            step(lambda e: e.tensor_scalar(TAs[:, ex, :], TAi[:, ex, :], 23, None, ALU.logical_shift_left))
            step(lambda e: e.tensor_scalar(
                B1S[:, ex * 8:(ex + 1) * 8], B1[:, ex, :], SC[:, ex, 2:3].bitcast(F32), None, ALU.mult))

        def parts(c, q):
            ex, i = c // 4, c % 4 - 2
            src, s = ST[:, i * 2048 + q * 512:i * 2048 + (q + 1) * 512], SC[:, ex, i:i + 1].bitcast(F32)
            if i == 0:
                o = ex * 8192 + q * 512
                return ex, i, src, s, W[:, o:o + 512], W[:, o + 2048:o + 2560]
            o = ex * 8192 + 4096 + q * 1024
            w = W[:, o:o + 1024].rearrange("p (f l n) -> p f l n", f=2, l=2)
            return ex, i, src.rearrange("p (f n) -> p f n", f=2), s, w[:, :, 0], w[:, :, 1]

        def wa(c, q):
            if c % 4 >= 2:
                while small:
                    small.pop(0)()
                ex, i, src, s, hi, lo = parts(c, q)
                tw["hi", c, q] = ac.do(lambda e: e.activation(hi, src, ACT.Copy, scale=s), tw["sc"], t_st[i])

        def wd(c, q):
            if c % 4 == 0:
                w_max(c // 4, 0, q)
            elif c % 4 == 1:
                if q < 2:
                    w_max(c // 4, 1, 2 * q)
                    w_max(c // 4, 1, 2 * q + 1)
                if q == 1:
                    w_scales(c // 4)
            else:
                ex, i, src, s, hi, lo = parts(c, q)
                a = ve.do(lambda e: e.scalar_tensor_tensor(lo, src, s, hi, ALU.mult, ALU.subtract),
                          tw["hi", c, q])
                if q == 3:
                    tw["w", ex] = a
                    if ex + 1 < E:
                        t_st[i] = load_w(ex + 1, i, a)

        a = ve.do(lambda e: e.tensor_reduce(BM[:, :], B1[:, :, :], X_AX, ALU.max, apply_absolute_value=True), t_b1)
        a = po.do(lambda e: e.partition_all_reduce(BMA[:, :], BM[:, :], 128, bass.bass_isa.ReduceOp.max), a)
        a = ve.do(lambda e: e.tensor_scalar(eb1[:, :], BMA[:, :].bitcast(I32), 23, None,
                                            ALU.logical_shift_right), a)
        a = ve.do(lambda e: e.tensor_scalar(eb1[:, :], eb1[:, :], 80, 240, ALU.max, ALU.min), a)
        t_eb1 = ve.do(lambda e: e.tensor_scalar(eb1[:, :], eb1[:, :], 1.0, None, ALU.add), a)

        t_free[R - 1] = (t_wph,)
        for c in range(2, R):
            t_x[c] = load_x(c)
        fns = dict(na=na, nn=nn, nb=nb, xh=xh, xl=xl, xt=xt, xTc=xTc, qk=qk, relu=relu, exp=exp, phi=phi,
                   hk=hk, lk=lk, ck=ck, hq=hq, lq=lq, cq=cq, vg=vg, vh=vh, vl=vl, lg=lg, trk=trk, kz=kz,
                   trq=trq, qs=qs, inter=inter, y=y, yh=yh, yl=yl, yt=yt, yTc=yTc, pr=pr, res=res, st=st)
        fns.update({"t32": t32, "t0": t0, "t1": t1, "t1a": t1a, "t2": t2})
        parted = dict(sc=sc, s=s_, sh=sh, sl=sl, pv=pv, wa=wa, wd=wd)
        course = sorted((place + c * PERIOD, name, c) for name, place in STEPS.items() for c in range(NC))
        for _, name, c in course:
            if name in ("t32", "t0", "t1", "t1a", "t2"):
                if c % CPB != CPB - 1:
                    fns[name](c)
            elif name in fns:
                fns[name](c)
            else:
                parted[name[:-1]](c, int(name[-1]))
            if small and name in ("phi", "lk", "lq", "kz", "vl", "s0", "s1", "s2", "s3", "y", "t32", "res", "wd2",
                                  "wd3", "nb", "na", "ck", "cq"):
                small.pop(0)()

        VA = ST[:, 0:2048]
        VX = ST[:, 2048:4096]
        R1 = VA[:, 0:256].rearrange("p (c e) -> p c e", e=E)
        R2 = VA[:, 256:512].rearrange("p (c e) -> p c e", e=E)
        O32 = VA[:, 512:768].rearrange("p (c e) -> p c e", e=E)
        TT = VA[:, 768:1024].rearrange("p (e c) -> p e c", e=E)
        PI = VA[:, 1024:1280].rearrange("p (e c) -> p e c", e=E)
        M1 = VA[:, 1280:1312]
        M2 = VA[:, 1312:1344]
        POS = VA[:, 1344:1376]
        POSI = VA[:, 1376:1408].bitcast(I32)
        SLI = VA[:, 1408:1440].bitcast(I32)
        PLI = VA[:, 1440:1472].bitcast(I32)
        NSI = VA[:, 1472:1480].bitcast(I32)
        NSF = VA[:, 1480:1488]
        CSF = VA[:, 1488:1496]
        BAS = VA[:, 1496:1504]
        O16 = VA[:, 1504:1632].bitcast(BF16)
        GE = VX[:, 0:NS * 8].rearrange("p (s e) -> p s e", e=8)
        ESF = VX[:, 320:320 + NS]
        IDF = VX[:, 384:384 + NS]
        EQS = VX[:, 512:512 + 32 * NS // 2].bitcast(BF16).rearrange("p (c s) -> p c s", c=32)
        AO = ar(1536, 2048).bitcast(BF16).rearrange("p (c n) -> p c n", c=32)
        BO = ar(3584, 1248).bitcast(BF16)[:, 0:32 * 2 * NS].rearrange(
            "p (c s) -> p c s", c=32)
        wt = cc(C_WT, 8).rearrange("p (o e) -> p o e", o=1).broadcast_to((128, NC, E))

        def bc(ap, n):
            return ap.rearrange("p (c o) -> p c o", o=1).broadcast_to((128, ap.shape[1], n))

        def bm(ap, n):
            return ap.rearrange("p (o c) -> p o c", o=1).broadcast_to((128, n, ap.shape[1]))

        LC = VA[:, 1632:2048]
        t_lc = sp.dma(lambda e: e.dma_start(LC, cst2), slot("k_lc"), tw["w", E - 1])
        fence = (g("lg", NC - 1), tw["w", E - 1])
        a = ve.do(lambda e: e.tensor_tensor(R1, L[:, :, :], bm(GBE[:, 1, :], NC), ALU.add), *fence)
        a = ve.do(lambda e: e.tensor_reduce(M1, R1, X_AX, ALU.max), a)
        a = ve.do(lambda e: e.tensor_tensor(R2, R1, bc(M1, E), ALU.is_equal), a)
        a = ve.do(lambda e: e.tensor_tensor(R2, R2, wt, ALU.mult), a)
        a = ve.do(lambda e: e.tensor_reduce(M2, R2, X_AX, ALU.max), a)
        a = ve.do(lambda e: e.tensor_tensor(O32, bc(M2, E), wt, ALU.is_equal), a)
        a = ve.do(lambda e: e.tensor_copy(O16, VA[:, 512:768]), a)
        pe.do(lambda e: e.matmul(PS[0][:, 0:256], tri16[:, :], O16, start=True, stop=True), a, t_tri, sig=False)
        b = pe.do(lambda e: e.matmul(PS[0][:, 256:512], one16[:, :], O16, start=True, stop=True), t_one)
        a = ve.do(lambda e: e.tensor_copy(TT, PS[0][:, 256:512].rearrange("p (c e) -> p e c", e=E)), b)
        a = ve.do(lambda e: e.tensor_tensor_scan(VA[:, 1024:1280], LC[:, D_RST:D_RST + 256], VA[:, 768:1024], 0.0,
                                                 ALU.mult, ALU.add), a, t_lc)
        a = ve.do(lambda e: e.tensor_scalar(NSI, PI[:, :, NC - 1], 127.0, None, ALU.add), a)
        a = ve.do(lambda e: e.tensor_scalar(NSI, NSI, 7, None, ALU.logical_shift_right), a)
        a = ve.do(lambda e: e.tensor_copy(NSF, NSI), a)
        a = ve.do(lambda e: e.tensor_tensor_scan(CSF, cc(C_ONE, 8), NSF, 0.0, ALU.mult, ALU.add), a)
        a = ve.do(lambda e: e.tensor_tensor(BAS, CSF, NSF, ALU.subtract), a)
        a = ve.do(lambda e: e.tensor_scalar(BAS, BAS, 128.0, None, ALU.mult), a)
        b = ve.do(lambda e: e.tensor_tensor(GE, bc(cc(C_SL, NS), 8), bm(CSF, NS), ALU.is_ge), a)
        b = ve.do(lambda e: e.tensor_reduce(ESF, GE[:, :, 0:7], X_AX, ALU.add), b)
        t_es = ve.do(lambda e: e.tensor_copy(es[:, :], ESF), b)
        a = ve.do(lambda e: e.tensor_tensor(PI, PI, TT, ALU.subtract))
        a = ve.do(lambda e: e.tensor_tensor(PI, PI, bc(BAS, NC), ALU.add), a)
        a = ve.do(lambda e: e.tensor_tensor(R1, PS[0][:, 0:256].rearrange("p (c e) -> p c e", e=E),
                                            VA[:, 1024:1280].rearrange("p (e c) -> p c e", e=E), ALU.add), a)
        a = ve.do(lambda e: e.tensor_tensor(R1, R1, O32, ALU.mult), a)
        a = ve.do(lambda e: e.tensor_reduce(POS, R1, X_AX, ALU.add), a)
        a = ve.do(lambda e: e.tensor_copy(POSI, POS), a)
        ve.do(lambda e: e.tensor_scalar(SLI, POSI, 7, None, ALU.logical_shift_right), a)
        a = ve.do(lambda e: e.tensor_scalar(PLI, POSI, 127, None, ALU.bitwise_and), a)
        a = ve.do(lambda e: e.tensor_copy(M1, SLI), a)
        a = ve.do(lambda e: e.tensor_copy(M2, PLI), a)
        a = ve.do(lambda e: e.tensor_tensor(EQS, bm(cc(C_SL, NS), NC), bc(M1, NS), ALU.is_equal), a)
        a1 = ve.do(lambda e: e.tensor_tensor(AO, bm(LC[:, D_P:D_P + 128], NC), bc(M2, 128), ALU.is_equal),
                   g("pv", (NC - 1, 3)))
        ve.do(lambda e: e.tensor_scalar(BO[:, :, 0:NS], EQS, cc(C_T, 1), None, ALU.mult), a,
              g("sl", (NC - 1, 3)))
        a = ve.do(lambda e: e.tensor_tensor(BO[:, :, NS:2 * NS], EQS, bc(LC[:, D_C32:D_C32 + 32], NS), ALU.mult), a)
        for c in range(NC):
            b = pe.do(lambda e, c=c: e.matmul(PS[1][:, 0:2 * NS], AO[:, c, :], BO[:, c, :],
                                              start=(c == 0), stop=(c == NC - 1)), a, sig=(c == NC - 1))
        a = ve.do(lambda e: e.tensor_scalar(IDF, PS[1][:, NS:2 * NS], 128.0, 4096.0, ALU.mult, ALU.add), b)
        a = ve.do(lambda e: e.tensor_tensor(IDF, IDF, PS[1][:, 0:NS], ALU.add), a)
        t_ids = ve.do(lambda e: e.tensor_copy(ids[:, :], IDF), a)

        NG = 4
        XG = [ar(i * 512, 512) for i in range(4)]
        B2 = ar(2048, 2048)
        OUT = [ar(4096 + i * 256, 256) for i in range(3)]
        RB = [ar(4864 + i * 256, 256) for i in range(3)]
        XH16 = [ar(5632 + i * 256, 256, F16) for i in range(2)]
        XT16 = [ar(6144 + i * 256, 256, F16) for i in range(2)]
        H32 = [ST[:, i * 1024:(i + 1) * 1024] for i in range(2)]
        HH = [ST[:, 2048 + i * 512:2560 + i * 512].bitcast(F16) for i in range(2)]
        HL = [ST[:, 3072 + i * 512:3584 + i * 512].bitcast(F16) for i in range(2)]
        k_b2 = slot("k_b2")
        k_g = [slot(f"k_g{i}") for i in range(4)]
        k_o = [slot(f"k_o{i}") for i in range(3)]
        t_b2 = sp.dma(lambda e: e.dma_start(B2, b2), k_b2, t_ids)
        scr_done = tuple(g("str", c) for c in range(NC - R, NC))
        t_z = []
        for i in range(4):
            t_z.append(ve.do(lambda e, i=i: e.memset(XG[i], 0.0), b, *scr_done))
        t_w = tw["w", E - 1]
        reg = {}

        def gather(s):
            tk["g", s] = po.dma(lambda e: e.indirect_dma_start(
                XG[s % NG], None, scr, bass.IndirectOffsetOnAxis(ids[:, s:s + 1], 0),
                bounds_check=NT - 1, oob_is_err=False), k_g[s % NG],
                t_ids, t_z[s % NG], *scr_done, g("xs", s - NG), g("rb", s - NG))

        def split_x(s):
            xg, x16 = XG[s % NG], XH16[s % 2]
            a = ac.do(lambda e: e.activation(x16[:, 0:256], xg[:, 0:256], ACT.Copy),
                      g("g", s), g("ptx", s - 2))
            tk["xs", s] = ve.do(lambda e: e.tensor_tensor(
                x16[:, 256:512], xg[:, 0:256], x16[:, 0:256], ALU.subtract), a)

            def addb(e):
                r = e.value_load(es[0:1, s:s + 1], min_val=0, max_val=E - 1)
                reg["ve", s] = r
                return e.tensor_tensor(RB[s % 3], xg[:, 256:512], B2[:, bass.ds(r * 256, 256)], ALU.add)

            tk["rb", s] = ve.do(addb, t_b2, t_es, g("g", s), g("o", s - 3))

        def pe_tx(s):
            pt = PS[6][:, 0:256].bitcast(F16)
            for i in range(4):
                a = pe.do(lambda e, i=i: e.transpose(pt[:, i * 128:(i + 1) * 128],
                                                     XH16[s % 2][:, i * 128:(i + 1) * 128], id16[:, :]),
                          t_id16, g("xs", s), g("tx", s - 1), sig=(i == 3))
            tk["ptx", s] = a
            tk["tx", s] = ac.do(lambda e: e.activation(XT16[s % 2], pt, ACT.Copy), a, g("pg1", s - 2))

        def pe_g1(s):
            xt = XT16[s % 2]

            def first(e):
                r = e.value_load(es[0:1, s:s + 1], min_val=0, max_val=E - 1)
                reg["pe", s] = r * 8192

            pe.wait(t_es)
            pe.items.append(first)
            ac.wait(t_es)

            def loada(e):
                reg["ac", s] = e.value_load(es[0:1, s:s + 1], min_val=0, max_val=E - 1)

            ac.items.append(loada)
            for f in range(8):
                bank = PS[2 * (s % 2) + f // 4]
                dst = bank[:, (f % 4) * 128:(f % 4 + 1) * 128]
                n = 0
                for k in range(2):
                    for wl, xl in ((0, 0), (0, 1), (1, 0)):
                        n += 1
                        off = wl * 2048 + k * 1024 + f * 128
                        a = pe.do(lambda e, off=off, xl=xl, k=k, n=n, dst=dst: e.matmul(
                            dst, W[:, off:off + 57472][:, bass.ds(reg["pe", s], 128)],
                            xt[:, xl * 256 + k * 128:xl * 256 + (k + 1) * 128], start=(n == 1), stop=(n == 6)),
                            g("tx", s), t_w, g("hr", (s - 2, 7)) if f // 4 else g("hr", (s - 2, 3)),
                            sig=(n == 6 and f % 4 == 3))
                if f % 4 == 3:
                    for ff in range(f - 3, f + 1):
                        src = bank[:, (ff % 4) * 128:(ff % 4 + 1) * 128]
                        tk["hr", (s, ff)] = ac.do(lambda e, ff=ff, src=src: e.activation(
                            H32[s % 2][:, ff * 128:(ff + 1) * 128], src, ACT.Relu,
                            bias=B1S[:, bass.ds(reg["ac", s] * 8 + ff, 1)],
                            scale=TAs[:, :, 0][:, bass.ds(reg["ac", s], 1)].bitcast(F32)),
                            a, g("hl", (s - 2, f // 4)), sig=(ff % 4 == 3))
                    q = f // 4
                    sl = slice(q * 512, (q + 1) * 512)
                    t = ve.do(lambda e, sl=sl: e.tensor_copy(HH[s % 2][:, sl], H32[s % 2][:, sl]),
                              tk["hr", (s, f)], g("pg2", s - 2))
                    tk["hl", (s, q)] = ve.do(lambda e, sl=sl: e.tensor_tensor(
                        HL[s % 2][:, sl], H32[s % 2][:, sl], HH[s % 2][:, sl], ALU.subtract), t)
                yield
            tk["pg1", s] = a

        def pe_g2(s):
            bank = PS[4 + s % 2]
            for f in range(8):
                off = 4096 + f * 512
                for src, w in ((HH, 512), (HL, 256)):
                    src = src[s % 2][:, f * 128:(f + 1) * 128]
                    a = pe.do(lambda e, off=off, src=src, w=w, f=f: e.matmul(
                        bank[:, 0:w], src, W[:, off:off + 57344 + w][:, bass.ds(reg["pe", s], w)],
                        start=(f == 0 and w == 512), stop=(f == 7), skip_group_check=True),
                        g("hl", (s, f // 4)), g("o", s - 2), sig=(f == 7 and w == 256))
                if f < 7:
                    yield
            tk["pg2", s] = a

            def half(lo, add):
                def fn(e):
                    r = reg["ve", s]
                    return e.scalar_tensor_tensor(
                        OUT[s % 3], bank[:, lo:lo + 256], TAs[:, :, 1][:, bass.ds(r, 1)].bitcast(F32), add,
                        ALU.mult, ALU.add)
                return fn

            b = ve.do(half(0, RB[s % 3]), a, g("rb", s), g("sc", s - 3))
            tk["o", s] = ve.do(half(256, OUT[s % 3]), b)
            tk["sc", s] = po.dma(lambda e: e.indirect_dma_start(
                outr, bass.IndirectOffsetOnAxis(ids[:, s:s + 1], 0), OUT[s % 3], None,
                bounds_check=NT - 1, oob_is_err=False), k_o[s % 3], tk["o", s])

        gather(0)
        gather(1)
        gather(2)
        split_x(0)
        pe_tx(0)
        split_x(1)
        for _ in pe_g1(0):
            pass
        pe_tx(1)
        for s in range(NS):
            if s + 3 < NS:
                gather(s + 3)
            if s + 2 < NS:
                split_x(s + 2)
            g1 = pe_g1(s + 1) if s + 1 < NS else iter(())
            g2 = pe_g2(s)
            for f in range(8):
                next(g1, None)
                if f == 6 and s + 2 < NS:
                    pe_tx(s + 2)
                next(g2, None)
            next(g1, None)
        po.wait(*(g("sc", s) for s in range(NS - 3, NS)))

        block = ctx.enter_context(nc.Block())
        block.tensor(pe.run)
        block.vector(ve.run)
        block.scalar(ac.run)
        block.gpsimd(po.run)
        block.sync(sp.run)


def kernel(**inputs):
    import numpy as np
    import concourse.bacc as _bacc
    from concourse import mybir as _mybir
    from concourse.bass_utils import run_bass_kernel_spmd as _run

    p = "L0_ffn_"
    x = np.ascontiguousarray(inputs["L0_attn_x"])
    wall = np.concatenate([inputs["L0_attn_w_attn"], inputs[p + "gate_w"]], 0)
    wall = np.ascontiguousarray(wall.T.reshape(2, 128, 776).transpose(1, 0, 2))
    wp = np.ascontiguousarray(np.asarray(inputs["L0_attn_w_proj"]).T.reshape(2, 128, 256).transpose(1, 0, 2))
    gb = np.ascontiguousarray(np.broadcast_to(np.asarray(inputs[p + "gate_b"])[None], (128, E)))
    eb = np.ascontiguousarray(np.broadcast_to(np.asarray(inputs[p + "expert_bias"])[None], (128, E)))
    w1 = np.ascontiguousarray(np.asarray(inputs[p + "w1"]).reshape(E, 2, 128, F).transpose(0, 2, 1, 3)
                              .reshape(E, 128, 2048))
    w2 = np.ascontiguousarray(np.asarray(inputs[p + "w2"]).reshape(E, 8, 128, D).transpose(0, 2, 1, 3)
                              .reshape(E, 128, 2048))
    b1 = np.ascontiguousarray(np.asarray(inputs[p + "b1"]).reshape(E, 8, 128).transpose(2, 0, 1))
    b2 = np.ascontiguousarray(np.broadcast_to(np.asarray(inputs[p + "b2"]).reshape(1, E * D), (128, E * D)))

    i = np.arange(128)
    cst = np.zeros((128, C_N), np.float32)
    cst[:, C_ID:C_ID + 128] = np.eye(128)
    cst[:, C_MASK:C_MASK + 128] = i[None, :] >= i[:, None]
    cst[:, C_PM:C_PM + 34] = (i[:, None] // 64) == (np.arange(34)[None] // 17)
    cst[:, C_ONE:C_ONE + 8] = 1.0
    cst[:, C_WT:C_WT + 8] = 8 - np.arange(8)[None]
    cst[:, C_SL:C_SL + NS] = np.arange(NS)[None]
    cst2 = np.zeros((128, D_N), np.float32)
    cst2[:, D_P:D_P + 128] = i[None]
    cst2[:, D_C32:D_C32 + 32] = np.arange(32)[None] - 32
    cst2[:, D_RST:D_RST + 256] = (np.arange(256) % 32 != 0)[None]
    tri = (i[:, None] < i[None, :]).astype(np.float32)
    cst[:, C_T] = i

    nc = _bacc.Bacc("TRN2", target_bir_lowering=False, num_devices=1)
    arrays, args = {}, []
    for name, a in (("x", x), ("wall", wall), ("wp", wp), ("gb", gb), ("eb", eb), ("w1", w1), ("b1", b1),
                    ("w2", w2), ("b2", b2), ("cst", cst), ("cst2", cst2), ("tri", tri)):
        arrays[f"in_{name}"] = a
        args.append(nc.dram_tensor(f"in_{name}", a.shape, _mybir.dt.from_np(a.dtype), kind="ExternalInput").ap())
    args.append(nc.dram_tensor("out_0", (B, T, D), _mybir.dt.float32, kind="ExternalOutput").ap())
    program(nc, *args)
    r = _run(nc, [arrays], core_ids=[0])
    return r.results[0]["out_0"]
```
